# Optimizing a Trainium2 kernel written in Bass

```python
import numpy as np
import jax
import jax.numpy as jnp

def _softmax(x, axis=-1):
    return jax.nn.softmax(x, axis=axis)

def _gelu(x):
    return jax.nn.gelu(x, approximate=True)

def _silu(x):
    return jax.nn.silu(x)

def _sigmoid(x):
    return jax.nn.sigmoid(x)

def _layernorm(x, axis=-1, eps=1e-05):
    m = jnp.mean(x, axis=axis, keepdims=True)
    v = jnp.var(x, axis=axis, keepdims=True)
    return (x - m) / jnp.sqrt(v + eps)

def _scatter_add(tgt, idx, src, axis=0):
    return tgt.at[idx].add(src)

def _segment_sum(src, seg, n):
    return jax.ops.segment_sum(src, seg, n)
kernel_name = 'mk_seq_preln_d1_jaxref_r8_0ff1d6'

def setup_inputs(seed: int=0):
    np.random.seed(seed)
    _w = jnp.asarray

    def _L0_attn_setup():
        import jax, jax.numpy as jnp
        import numpy as np
        import math
        HIDDEN = 128
        HEADS = 16
        HEAD_DIM = HIDDEN // HEADS
        NUM_FEATURES = 64
        B, N = (4, 512)

        def _feature_map(x, rf):
            proj = jnp.einsum('bhnd,fd->bhnf', x, rf) / jnp.sqrt(jnp.float32(NUM_FEATURES))
            norm = jnp.linalg.norm(x, axis=-1, keepdims=True)
            return jnp.exp(proj - norm)
        key = jax.random.key(seed)
        ks = jax.random.split(key, 5)
        x = jax.random.normal(ks[0], (B, N, HIDDEN), dtype=jnp.float32)
        w_qkv = jax.random.normal(ks[1], (3 * HIDDEN, HIDDEN), dtype=jnp.float32) / math.sqrt(HIDDEN)
        w_out = jax.random.normal(ks[2], (HIDDEN, HIDDEN), dtype=jnp.float32) / math.sqrt(HIDDEN)
        b_out = jnp.zeros((HIDDEN,), dtype=jnp.float32)
        random_features = jax.random.normal(ks[3], (NUM_FEATURES, HEAD_DIM), dtype=jnp.float32)
        return {'x': x, 'w_qkv': w_qkv, 'w_out': w_out, 'b_out': b_out, 'random_features': random_features}
    _L0_attn_in = _L0_attn_setup()

    def _L0_ffn_setup():
        import jax, jax.numpy as jnp
        import numpy as np
        NUM_EXPERTS = 8
        TOP_K = 2
        DIM = 128
        HIDDEN = 512
        BATCH, SEQ = (16, 32)
        key = jax.random.key(seed)
        k1, k2, k3, k4, k5 = jax.random.split(key, 5)
        scale = 1.0 / np.sqrt(DIM)
        return {'hidden_states': jax.random.normal(k1, (BATCH, SEQ, DIM), dtype=jnp.float32), 'gate_w': jax.random.normal(k2, (NUM_EXPERTS, DIM), dtype=jnp.float32) * scale, 'w1': jax.random.normal(k3, (NUM_EXPERTS, HIDDEN, DIM), dtype=jnp.float32) * scale, 'w3': jax.random.normal(k4, (NUM_EXPERTS, HIDDEN, DIM), dtype=jnp.float32) * scale, 'w2': jax.random.normal(k5, (NUM_EXPERTS, DIM, HIDDEN), dtype=jnp.float32) * (1.0 / np.sqrt(HIDDEN))}
    _L0_ffn_in = _L0_ffn_setup()
    _d = {'L0_attn_x': _L0_attn_in['x'], 'L0_attn_w_qkv': _L0_attn_in['w_qkv'], 'L0_attn_w_out': _L0_attn_in['w_out'], 'L0_attn_b_out': _L0_attn_in['b_out'], 'L0_attn_random_features': _L0_attn_in['random_features'], 'L0_ffn_gate_w': _L0_ffn_in['gate_w'], 'L0_ffn_w1': _L0_ffn_in['w1'], 'L0_ffn_w3': _L0_ffn_in['w3'], 'L0_ffn_w2': _L0_ffn_in['w2']}
    _x0 = _d['L0_attn_x']
    _d['L0_attn_x'] = jax.random.normal(jax.random.fold_in(jax.random.key(seed), 1), (32, 256, 128), dtype=_x0.dtype)
    del _x0
    return _d

def reference(L0_attn_x, L0_attn_w_qkv, L0_attn_w_out, L0_attn_b_out, L0_attn_random_features, L0_ffn_gate_w, L0_ffn_w1, L0_ffn_w3, L0_ffn_w2):

    def _L0_attn_ref(x, w_qkv, w_out, b_out, random_features):
        import jax, jax.numpy as jnp
        import numpy as np
        import math
        HIDDEN = 128
        HEADS = 16
        HEAD_DIM = HIDDEN // HEADS
        NUM_FEATURES = 64
        B, N = (4, 512)

        def _feature_map(x, rf):
            proj = jnp.einsum('bhnd,fd->bhnf', x, rf) / jnp.sqrt(jnp.float32(NUM_FEATURES))
            norm = jnp.linalg.norm(x, axis=-1, keepdims=True)
            return jnp.exp(proj - norm)
        b, n, _ = x.shape
        qkv = jnp.einsum('bnh,oh->bno', x, w_qkv)
        qkv = qkv.reshape(b, n, 3, HEADS, HEAD_DIM)
        qkv = jnp.transpose(qkv, (2, 0, 3, 1, 4))
        q, k, v = (qkv[0], qkv[1], qkv[2])
        q_prime = _feature_map(q, random_features)
        k_prime = _feature_map(k, random_features)
        kv = jnp.einsum('bhnf,bhnd->bhfd', k_prime, v)
        normalizer = jnp.einsum('bhnf,bhf->bhn', q_prime, k_prime.sum(axis=2))
        out = jnp.einsum('bhnf,bhfd->bhnd', q_prime, kv)
        out = out / (normalizer[..., None] + 1e-06)
        out = jnp.transpose(out, (0, 2, 1, 3)).reshape(b, n, HIDDEN)
        return jnp.einsum('bnh,oh->bno', out, w_out) + b_out

    def _L0_ffn_ref(hidden_states, gate_w, w1, w3, w2):
        import jax, jax.numpy as jnp
        import numpy as np
        NUM_EXPERTS = 8
        TOP_K = 2
        DIM = 128
        HIDDEN = 512
        BATCH, SEQ = (16, 32)
        B, S, D = hidden_states.shape
        x = hidden_states.reshape(-1, D)
        router_logits = x @ gate_w.T
        probs = jax.nn.softmax(router_logits.astype(jnp.float32), axis=-1)
        routing_weights, selected_experts = jax.lax.top_k(probs, TOP_K)
        routing_weights = routing_weights / routing_weights.sum(axis=-1, keepdims=True)
        routing_weights = routing_weights.astype(x.dtype)
        coef = (jax.nn.one_hot(selected_experts, NUM_EXPERTS, dtype=x.dtype) * routing_weights[..., None]).sum(axis=1)
        h1 = jnp.einsum('td,ehd->teh', x, w1)
        h3 = jnp.einsum('td,ehd->teh', x, w3)
        act = jax.nn.silu(h1) * h3
        expert_out = jnp.einsum('teh,edh->ted', act, w2)
        out = jnp.einsum('ted,te->td', expert_out, coef)
        return out.reshape(B, S, D)
    x = L0_attn_x
    x = x + _L0_attn_ref(_layernorm(x, axis=-1), L0_attn_w_qkv, L0_attn_w_out, L0_attn_b_out, L0_attn_random_features)
    x = x + _L0_ffn_ref(_layernorm(x, axis=-1), L0_ffn_gate_w, L0_ffn_w1, L0_ffn_w3, L0_ffn_w2)
    return x

_drawn_inputs = setup_inputs


def setup_inputs(seed=0):
    import zlib

    import numpy as np

    out = dict(_drawn_inputs(seed))
    spreads = {'L0_attn_b_out': (0.0, 0.1)}
    factors = {'L0_attn_random_features': 3.48}
    for name, (base, spread) in spreads.items():
        noise = np.random.default_rng([zlib.crc32(name.encode()), seed]).standard_normal(out[name].shape)
        drawn = base * np.exp(spread * noise) if base else spread * noise
        out[name] = jnp.asarray(drawn.astype(out[name].dtype))
    for name, factor in factors.items():
        out[name] = (out[name] * factor).astype(out[name].dtype)
    return out
```

```python
from contextlib import ExitStack

import concourse.bass as bass
from concourse import mybir

F32, F16, BF16 = mybir.dt.float32, mybir.dt.float16, mybir.dt.bfloat16
I32, U32 = mybir.dt.int32, mybir.dt.uint32
ACT, ALU, AX = mybir.ActivationFunctionType, mybir.AluOpType, mybir.AxisListType

P = 128
T = 8192
D = 128
H, HD, F = 16, 8, 64
NT = T // P
NB = 32
E, HID, TOPK = 8, 512, 2
SLOTS = 256
NX = T * TOPK // SLOTS + E
CAP = T + SLOTS
ROW = 264
ID = 256
PAD_ID = T * TOPK
W_SCALE = 16.0
Z_LN = 8 * 0.6931471805599453
Z2 = 65536.0
LN_EPS = 1e-5
WCH = E * 3 * HID // NB
LAG = 4
GUESS = float(0x5F3759DF)


def need(eng, sem, value):
    if isinstance(value, int) and value <= 0:
        return
    eng.wait_ge(sem, value)


def wait_apart(eng, passed, sem, value):
    if isinstance(value, int):
        return need(eng, sem, value)
    eng.wait_ge(sem, value).then_inc(passed, 1)


def pipeline(eng, stages, last=LAG, n=NB):
    for it in range(last + 2):
        for lag, stage in stages:
            if it - lag >= 0:
                stage(it - lag, (it - lag) % 2)
    with eng.Fori(last // 2 + 1, n // 2) as i:
        for u in range(2):
            for lag, stage in stages:
                stage(i * 2 + (u - lag), (u - lag) % 2)
    for it in range(n, n + last):
        for lag, stage in stages:
            if it - lag < n:
                stage(it - lag, (it - lag) % 2)


def reads_before(uses, k, b):
    it = b + uses[k][0]
    if isinstance(b, int):
        return sum(n * min(max(it - lag + (j < k), 0), NB) for j, (lag, n) in enumerate(uses))
    return it * sum(n for _, n in uses) + sum(n * ((j < k) - lag) for j, (lag, n) in enumerate(uses))


BANK_T = [(2, 1), (2, 1), (0, 1), (3, 1), (4, 1)]
T_EXTQ, T_EXTK, T_LN1, T_ATT, T_LN2 = range(5)
BANK_Q = [(3, 1), (1, 1)]
Q_WOUT, Q_QKV = range(2)
BANK_M = [(3, 1), (4, 1), (2, 1), (4, 1)]
M_OUT, M_RT, M_KV, M_POS = range(4)


def build(nc, x, wa, bout, rft, rfc, wffn, mask, out, xs, planes):
    with ExitStack() as ctx:
        def sb(name, shape, dt):
            return ctx.enter_context(nc.sbuf_tensor(name, shape, dt))

        def psum(name, shape, dt):
            return ctx.enter_context(nc.psum_tensor(name, shape, dt))

        def sem(name):
            return ctx.enter_context(nc.semaphore(name))

        ident = sb("ident", [P, P], F16)
        tri = sb("tri", [P, P], F16)
        ones = sb("ones", [P, P], F16)
        wa_f = sb("wa_f", [P, 520], F32)
        wa_hi = sb("wa_hi", [P, 520], F16)
        wa_lo = sb("wa_lo", [P, 520], F16)
        rf_f = sb("rf_f", [P, 4 * F], F32)
        rf = sb("rf", [P, 4 * F], F16)
        b_bc = sb("b_bc", [P, D], F32)
        kvmask = sb("kvmask", [P, 18], F32)
        rank = sb("rank", [P, E], F32)
        ebase = sb("ebase", [P, E], F32)
        ids = sb("ids", [P, TOPK, NT], I32)
        w_st = sb("w_st", [P, 2, WCH], F32)
        w_hi = sb("w_hi", [P, E * 3 * HID], F16)
        w_lo = sb("w_lo", [P, E * 3 * HID], F16)

        xall = sb("xall", [P, NT, D], F32)
        gap = sb("gap", [P, NT], F32)
        mcum = sb("mcum", [P, E], F16)

        bn = sb("bn", [P, 2, 2, 6], F32)
        mv1 = sb("mv1", [P, 2, 2, 2], F32)
        nt1 = sb("nt1", [P, 2, 4, 2], F32)
        xn_f = sb("xn_f", [P, 2, 2, D], F32)
        xn_s = sb("xn_s", [P, 2, 2, 2, D], F16)
        xT = sb("xT", [P, 2, 2, 256], F16)
        ext = sb("ext", [P, 2, 2, 8, P], F16)
        sq = sb("sq", [P, 2, 2, 256], F32)
        nrm = sb("nrm", [P, 2, 6, 64], F32)
        vx = sb("vx", [P, 2, 2, 2, 8, 17], F16)
        extT = sb("extT", [P, 2, 8, 256], F16)
        eq = sb("eq", [P, 2, 2, 1024], F32)
        eq_lo = sb("eq_lo", [P, 2, 2, 1024], F16)
        ek = sb("ek", [P, 2, 1024], F32)
        ek_lo = sb("ek_lo", [P, 2, 1024], F16)
        kvm = sb("kvm", [P, 8, 18], F32)
        kvr = sb("kvr", [P, 8, 18], F32)
        kvp = sb("kvp", [P, 3, 8, 18], BF16)
        den = sb("den", [P, 16, 2], F32)
        rden = sb("rden", [P, 16, 2], F32)
        at_f = sb("at_f", [P, 2, D], F32)
        at_s = sb("at_s", [P, 2, 2, D], F16)
        atT = sb("atT", [P, 2, 256], F16)
        mv2 = sb("mv2", [P, 2, 2, 2], F32)
        nt2 = sb("nt2", [P, 2, 4, 2], F32)
        x2_f = sb("x2_f", [P, 2, D], F32)
        rows = sb("rows", [P, 2, TOPK, 2, ROW], F16)
        x2T = sb("x2T", [P, 2, 256], F16)
        lg = sb("lg", [P, 2, E], F32)
        lg2 = sb("lg2", [P, 2, E], F32)
        cand = sb("cand", [P, 2, 2, 2, E], F32)
        top = sb("top", [P, 4, 2], F32)
        pick = sb("pick", [P, 2, 2, E], F32)
        both = sb("both", [P, 2, 2, E], F16)
        cum1 = sb("cum1", [P, E], F16)
        free = sb("free", [P, 1], F32)
        zbias = sb("zbias", [P, 1], F32)
        where = sb("where", [P, 2, E], F32)
        hit = sb("hit", [P, 2, 2, E], F32)
        slot_f = sb("slot_f", [P, 4], F32)
        slot = sb("slot", [P, 2, 4], U32)

        pad = sb("pad", [P, 2, ROW], F16)
        cnt = sb("cnt", [P, E], F32)
        cnt_i = sb("cnt_i", [P, E], I32)
        up_i = sb("up_i", [P, 2, E], I32)
        ntile = sb("ntile", [P, E], F32)
        ends = sb("ends", [P, E], F32)
        skip = sb("skip", [P, E], F32)
        tnum = sb("tnum", [P, NX], F32)
        past = sb("past", [P, NX, E], F32)
        jump = sb("jump", [P, NX, E], F32)
        tab_f = sb("tab_f", [P, 2, 2, NX], F32)
        tab = sb("tab", [P, 2, NX], I32)
        coef = sb("coef", [P, 4, NT], F32)

        xl = sb("xl", [P, 2, 2, ROW], F16)
        xlT = sb("xlT", [P, 2, 2, SLOTS], F16)
        gate = sb("gate", [P, 2, 512], F32)
        act_f = sb("act_f", [P, 2, 512], F32)
        act_hi = sb("act_hi", [P, 2, 4, SLOTS], F16)
        act_lo = sb("act_lo", [P, 2, 4, SLOTS], F16)
        y = sb("y", [P, 2, 2, D], F32)
        row_id = sb("row_id", [P, NX, 2], I32)
        put_id = sb("put_id", [P, 2, 2], I32)

        pl = eq[:].rearrange("p a k (t d) -> p a k t d", t=8)

        z = psum("z", [P, 2, 1024], F32)
        bT = psum("bT", [P, 1024], F16)
        bQ = psum("bQ", [P, 2, 512], F32)
        bM = psum("bM", [P, 512], F32)
        m_out = bM[:, 0:288].rearrange("p (t j c) -> p t j c", t=2, j=8)
        m_kv = bM[:, 288:424].rearrange("p (j c) -> p j c", j=8)
        m_rt = bM[:, 424:440].rearrange("p (t e) -> p t e", t=2)
        m_pos = bM[:, 440:456].rearrange("p (t e) -> p t e", t=2)

        dve_passed, pool_passed = sem("dve_passed"), sem("pool_passed")
        xload = [sem(f"xload{i}") for i in range(2)]
        wload = [sem(f"wload{i}") for i in range(2)]
        cload = sem("cload")
        rload = sem("rload")
        pset = sem("pset")
        wa_hi_set, wa_lo_set, rf_hi_set, rf_set = sem("wa_hi_set"), sem("wa_lo_set"), sem("rf_hi_set"), sem("rf_set")
        wsplit_hi, wsplit_lo = sem("wsplit_hi"), sem("wsplit_lo")
        ln1, xn_set, xnhi_set, xnlo_set, bias_set = sem("ln1"), sem("xn_set"), sem("xnhi_set"), sem("xnlo_set"), sem("bias_set")
        t_ln1, t_extq, t_extk, t_att, t_ln2 = (sem(n) for n in ("t_ln1", "t_extq", "t_extk", "t_att", "t_ln2"))
        t_read = sem("t_read")
        q_done, q_read, qhi_set, qlo_set, slab2_set, sq_set, ss_set = (
            sem(n) for n in ("q_done", "q_read", "qhi_set", "qlo_set", "slab2_set", "sq_set", "ss_set"))
        v_set, nrm_st, nrm_set = sem("v_set"), sem("nrm_st"), sem("nrm_set")
        z_done, z_exp, eklo_set, eqlo_set = sem("z_done"), sem("z_exp"), sem("eklo_set"), sem("eqlo_set")
        kv_done, kv_st, kv_set = sem("kv_done"), sem("kv_st"), sem("kv_set")
        m_read = sem("m_read")
        o_done, at_st, athi_set, atlo_set = sem("o_done"), sem("at_st"), sem("athi_set"), sem("atlo_set")
        w_done, x1_set, ln2_st, ln2_set = sem("w_done"), sem("x1_set"), sem("ln2_st"), sem("ln2_set")
        x2_set, x2hi_set, x2lo_set, rows_set = sem("x2_set"), sem("x2hi_set"), sem("x2lo_set"), sem("rows_set")
        rt_done, rt_st, both_set, pos_done, slot_set = (
            sem(n) for n in ("rt_done", "rt_st", "both_set", "pos_done", "slot_set"))
        cum_set, cum_st, zb_set = sem("cum_set"), sem("cum_st"), sem("zb_set")
        scat = [sem(f"scat{i}") for i in range(2)]

        cnt_done, ph2, cnt_set, tab_set, coef_e, coef_set, tail = (
            sem(n) for n in ("cnt_done", "ph2", "cnt_set", "tab_set", "coef_e", "coef_set", "tail"))
        xl_load = [sem(f"xl_load{i}") for i in range(2)]
        y_scat = [sem(f"y_scat{i}") for i in range(2)]
        id_kept = sem("id_kept")
        xl_turned, xlT_set, h_done, silu_set, act_set, acthi_set, actlo_set, y_done, y_set = (
            sem(n) for n in ("xl_turned", "xlT_set", "h_done", "silu_set", "act_set", "acthi_set", "actlo_set",
                             "y_done", "y_set"))
        pl_load = [sem(f"pl_load{i}") for i in range(2)]
        sum1_set, sum2_set, stored = sem("sum1_set"), sem("sum2_set"), sem("stored")

        bf_hi = lambda a: a.bitcast(BF16).rearrange("p (n two) -> p two n", two=2)[:, 1, :]

        with nc.Block() as block:
            @block.sync
            def _(sp):
                sp.dma_start(wa_f[:], wa).then_inc(cload, 16)
                sp.dma_start(b_bc[:], bout).then_inc(cload, 16)
                sp.dma_start(kvmask[:], mask).then_inc(cload, 16)
                sp.dma_start(rf_f[:], rfc).then_inc(rload, 16)
                sp.wait_ge(rload, 16)
                for s in range(3):
                    for h in range(4):
                        r0 = 32 * s + 8 * h
                        sp.dma_start(rf_f[r0:r0 + 8, F * h:F * h + F], rft).then_inc(rload, 16)

                def load(b, p):
                    need(sp, xload[p], 8 * (b - p))
                    sp.dma_start(xall[:, bass.ds(b * 2, 2), :], x[:, bass.ds(b * 2, 2), :]).then_inc(xload[p], 16)
                    need(sp, wsplit_lo, b - 1)
                    need(sp, wsplit_hi, b - 1)
                    sp.dma_start(w_st[:, p, :], wffn[:, bass.ds(b * WCH, WCH)]).then_inc(wload[p], 16)

                for b in range(2):
                    load(b, b)
                with sp.Fori(1, NB // 2) as i:
                    for u in range(2):
                        load(i * 2 + u, u)

                sp.wait_ge(pset, 17)
                sp.dma_start(xs[E * CAP:E * CAP + SLOTS, :].rearrange("(h p) r -> p h r", p=P),
                             pad[:]).then_inc(tail, 16)
                sp.wait_ge(cnt_set, 1)
                for e in range(E):
                    n = nc.values_load(cnt_i[0:1, e:e + 1], engines=[mybir.EngineType.SP], min_val=0, max_val=T,
                                       skip_runtime_bounds_check_because="counts of tokens")
                    sp.dma_start(xs[bass.ds(n + e * CAP, SLOTS), :].rearrange("(h p) r -> p h r", p=P),
                                 pad[:]).then_inc(tail, 16)
                sp.wait_ge(tail, 16 * (E + 1))
                sp.wait_ge(tab_set, 1)
                for p in range(2):
                    sp.wait_ge(scat[p], 64 * NB // 2)

                def fetch(t, p):
                    need(sp, xl_turned, t - 1)
                    need(sp, id_kept, t - 1)
                    r = nc.values_load(tab[0:1, 1, bass.ds(t, 1)], engines=[mybir.EngineType.SP], min_val=0,
                                       max_val=E * CAP, skip_runtime_bounds_check_because="clamped to the last tile")
                    sp.dma_start(xl[:, p], xs[bass.ds(r, SLOTS), :].rearrange("(h p) r -> p h r", p=P)).then_inc(
                        xl_load[p], 16)

                pipeline(sp, [(0, fetch)], 0, NX)
                for p in range(2):
                    sp.wait_ge(y_scat[p], 32 * NX // 2)

                def fetch_rows(g, p):
                    need(sp, sum2_set, 8 * (g - 1))
                    for k in range(TOPK):
                        sp.dma_start(pl[:, p, k], planes[bass.ds(g * 1024 + k * T, 1024), :].rearrange(
                            "(t p) d -> p t d", p=P)).then_inc(pl_load[p], 16)

                pipeline(sp, [(0, fetch_rows)], 0, 8)

            def landed(b, p):
                return 8 * (b - p) + 16

            @block.gpsimd
            def _(pool):
                nc.gpsimd.memset(ident[:], 0.0).then_inc(pset, 1)
                nc.gpsimd.memset(tri[:], 0.0).then_inc(pset, 1)
                nc.gpsimd.memset(ones[:], 1.0).then_inc(pset, 1)
                nc.gpsimd.memset(mcum[:], 0.0).then_inc(pset, 1)
                nc.gpsimd.memset(ext[:, 0], 0.0).then_inc(pset, 1)
                nc.gpsimd.memset(ext[:, 1], 0.0).then_inc(pset, 1)
                nc.gpsimd.memset(vx[:, :, :, 0, :, 16:17], 1.0).then_inc(pset, 1)
                nc.gpsimd.memset(vx[:, :, :, 1, :, 16:17], 0.0).then_inc(pset, 1)
                nc.gpsimd.memset(rows[:], 0.0).then_inc(pset, 1)
                nc.gpsimd.iota(ids[:], [[T, TOPK], [P, NT]], base=0, channel_multiplier=1).then_inc(pset, 1)
                nc.gpsimd.iota(rank[:], [[-1, E]], base=E, channel_multiplier=0,
                               allow_small_or_imprecise_dtypes=True).then_inc(pset, 1)
                nc.gpsimd.iota(ebase[:], [[CAP, E]], base=0, channel_multiplier=0,
                               allow_small_or_imprecise_dtypes=True).then_inc(pset, 1)
                nc.gpsimd.iota(tnum[:], [[1, NX]], base=0, channel_multiplier=0,
                               allow_small_or_imprecise_dtypes=True).then_inc(pset, 1)
                nc.gpsimd.memset(pad[:], 0.0).then_inc(pset, 1)
                pool.wait_ge(pset, 14)
                nc.gpsimd.memset(pad[:, :, ID:ID + 2].bitcast(I32), PAD_ID).then_inc(pset, 1)
                nc.gpsimd.affine_select(out=ident[:], in_=ident[:], compare_op=ALU.not_equal, fill=1.0, base=0,
                                        pattern=[[-1, P]], channel_multiplier=1).then_inc(pset, 1)
                nc.gpsimd.affine_select(out=tri[:], in_=tri[:], compare_op=ALU.is_ge, fill=1.0, base=0,
                                        pattern=[[-1, P]], channel_multiplier=1).then_inc(pset, 1)

                def rsqrt(a, y, t, w, st, base):
                    nc.gpsimd.tensor_scalar(y.bitcast(I32), a.bitcast(I32), -0.5, GUESS, ALU.mult,
                                            ALU.add).then_inc(st, 1)
                    for k in range(3):
                        pool.wait_ge(st, base + 4 * k + 1)
                        nc.gpsimd.tensor_tensor(out=t, in0=a, in1=y, op=ALU.mult).then_inc(st, 1)
                        pool.wait_ge(st, base + 4 * k + 2)
                        nc.gpsimd.tensor_tensor(out=w, in0=t, in1=y, op=ALU.mult).then_inc(st, 1)
                        wait_apart(pool, pool_passed, st, base + 4 * k + 3)
                        nc.gpsimd.tensor_scalar(t, w, -0.5, 1.5, ALU.mult, ALU.add).then_inc(st, 1)
                        pool.wait_ge(st, base + 4 * k + 4)
                        nc.gpsimd.tensor_tensor(out=y, in0=y, in1=t, op=ALU.mult).then_inc(st, 1)

                def norms(b, p):
                    wait_apart(pool, pool_passed, ss_set, b + 1)
                    n = nrm[:, p]
                    rsqrt(n[:, 0], n[:, 1], n[:, 2], n[:, 3], nrm_st, b * 15)
                    pool.wait_ge(nrm_st, b * 15 + 13)
                    nc.gpsimd.tensor_tensor(out=n[:, 4], in0=n[:, 0], in1=n[:, 1], op=ALU.mult).then_inc(nrm_st, 1)
                    need(pool, t_extk, b - 1)
                    wait_apart(pool, pool_passed, nrm_st, b * 15 + 14)
                    e = ext[:, p].rearrange("p t g c -> p (t g) c")
                    nv = n[:, 4].rearrange("p (tg h) -> p tg h", h=4)
                    nc.gpsimd.tensor_copy(e[:, :, 96:100], nv).then_inc(nrm_st, 1)
                    wait_apart(pool, pool_passed, nrm_st, b * 15 + 15)
                    nc.gpsimd.tensor_tensor(out=e[:, :, 100:104], in0=nv, in1=e[:, :, 96:100],
                                            op=ALU.subtract).then_inc(nrm_set, 1)

                def bias(b, p):
                    pool.wait_ge(xn_set, 2 * (b + 1))
                    for t in range(2):
                        v = xall[:, bass.ds(b * 2 + t, 1), :]
                        ins = nc.gpsimd.tensor_tensor(out=v, in0=v, in1=b_bc[:].rearrange("p (o d) -> p o d", o=1),
                                                      op=ALU.add)
                    ins.then_inc(bias_set, 1)

                def ln2(b, p):
                    wait_apart(pool, pool_passed, ln2_st, 5 * (b + 1))
                    n = nt2[:, p]
                    rsqrt(n[:, 0], n[:, 1], n[:, 2], n[:, 3], ln2_set, b * 13)

                def scatter(b, p):
                    pool.wait_ge(slot_set, b + 1)
                    wait_apart(pool, pool_passed, rows_set, 3 * (b + 1))
                    for k in range(TOPK):
                        for t in range(2):
                            pool.indirect_dma_start(
                                out=xs[:, :], out_offset=bass.IndirectOffsetOnAxis(
                                    ap=slot[:, p, 2 * k + t:2 * k + t + 1], axis=0),
                                in_=rows[:, p, k, t, :], in_offset=None).then_inc(scat[p], 16)

                pool.wait_ge(cload, 48)
                pipeline(pool, [(0, bias), (3, ln2), (1, norms), (4, scatter)])

                def put(t, p):
                    wait_apart(pool, pool_passed, y_set, 2 * (t + 1))
                    for h in range(2):
                        pool.indirect_dma_start(
                            out=planes[:, :], out_offset=bass.IndirectOffsetOnAxis(
                                ap=put_id[:, p, h:h + 1].bitcast(U32), axis=0),
                            in_=y[:, p, h, :], in_offset=None, bounds_check=TOPK * T - 1,
                            oob_is_err=False).then_inc(y_scat[p], 16)

                pool.wait_ge(tail, 16 * (E + 1))
                pipeline(pool, [(2, put)], 2, NX)

            @block.scalar
            def _(act):
                act.wait_ge(cload, 48)
                nc.scalar.activation(wa_hi[:], wa_f[:], ACT.Copy, scale=W_SCALE).then_inc(wa_hi_set, 1)
                act.wait_ge(rload, 16 * 13)
                nc.scalar.activation(rf[:], rf_f[:], ACT.Copy).then_inc(rf_hi_set, 1)

                def xn_hi(b, p):
                    act.wait_ge(xn_set, 2 * (b + 1))
                    need(act, t_ln1, b - 1)
                    nc.scalar.activation(xn_s[:, p, 0], xn_f[:, p], ACT.Copy).then_inc(xnhi_set, 1)

                def xt_copy(b, p):
                    act.wait_ge(t_ln1, b + 1)
                    need(act, q_done, 2 * (b - 1))
                    nc.scalar.activation(xT[:, p].rearrange("p a n -> p (a n)"), bT[:, 0:512],
                                         ACT.Copy).then_inc(t_read, 1)

                def qkv_hi(b, p):
                    for t in range(2):
                        act.wait_ge(q_done, 2 * b + t + 1)
                        if t == 0:
                            need(act, t_extk, b - 1)
                            need(act, kv_done, b - 1)
                            need(act, ss_set, b - 1)
                        qk = bQ[:, t, 0:256]
                        nc.scalar.activation(ext[:, p, t, :, 0:32], qk.rearrange("p (g c) -> p g c", g=8),
                                             ACT.Copy).then_inc(qhi_set, 1)
                        nc.scalar.activation(sq[:, p, t, :], qk, ACT.Square).then_inc(sq_set, 1)
                        nc.scalar.activation(vx[:, p, t, 0, :, 0:16],
                                             bQ[:, t, 256:384].rearrange("p (j c) -> p j c", j=8),
                                             ACT.Copy).then_inc(v_set, 1)

                def ext_copy(half, done):
                    def stage(b, p):
                        act.wait_ge(done, b + 1)
                        if half == 0:
                            need(act, z_done, 4 * (b - 1))
                        nc.scalar.activation(extT[:, p, 4 * half:4 * half + 4, :].rearrange("p g n -> p (g n)"),
                                             bT[:], ACT.Copy).then_inc(t_read, 1)
                    return stage

                def exp(k):
                    def stage(b, p):
                        act.wait_ge(z_done, 4 * b + k + 1)
                        if k < 2:
                            need(act, o_done, b - 1)
                            need(act, eqlo_set, 2 * (b - 2) + 1 + k)
                            dst = eq[:, p, k]
                        else:
                            need(act, kv_done, b)
                            dst = ek[:, k - 2]
                        nc.scalar.activation(dst, z[:, k % 2], ACT.Exp, bias=zbias[:, 0:1],
                                             scale=1.0 / (8 * W_SCALE)).then_inc(z_exp, 1)
                    return stage

                def att_hi(b, p):
                    act.wait_ge(at_st, 3 * (b + 1))
                    need(act, t_att, b)
                    nc.scalar.activation(at_s[:, 0], at_f[:], ACT.Copy).then_inc(athi_set, 1)

                def att_copy(b, p):
                    act.wait_ge(t_att, b + 1)
                    need(act, w_done, b)
                    nc.scalar.activation(atT[:].rearrange("p a n -> p (a n)"), bT[:, 0:512],
                                         ACT.Copy).then_inc(t_read, 1)

                def x2_hi(b, p):
                    act.wait_ge(x2_set, 2 * (b + 1))
                    need(act, scat[p], 32 * (b - p))
                    need(act, rows_set, 3 * (b - 1))
                    nc.scalar.activation(rows[:, p, 0, :, 0:D], x2_f[:], ACT.Copy).then_inc(x2hi_set, 1)

                def x2_copy(b, p):
                    act.wait_ge(t_ln2, b + 1)
                    need(act, rt_done, b)
                    nc.scalar.activation(x2T[:].rearrange("p a n -> p (a n)"), bT[:, 0:512],
                                         ACT.Copy).then_inc(t_read, 1)

                def w_part(b, p):
                    act.wait_ge(wload[p], landed(b, p))
                    nc.scalar.activation(w_hi[:, bass.ds(b * WCH, WCH)], w_st[:, p, :], ACT.Copy,
                                         scale=W_SCALE).then_inc(wsplit_hi, 1)

                act.wait_ge(zb_set, 1)
                pipeline(act, [(4, x2_hi), (2, ext_copy(0, t_extq)), (2, ext_copy(1, t_extk)), (0, xn_hi), (2, exp(0)),
                               (0, xt_copy), (2, exp(1)), (3, att_hi), (3, att_copy), (4, x2_copy), (2, exp(2)),
                               (2, exp(3)), (1, qkv_hi), (0, w_part)])

                def silu(k):
                    def stage(t, p):
                        act.wait_ge(h_done, 2 * t + k + 1)
                        need(act, act_set, 2 * t + k - 1)
                        nc.scalar.activation(gate[:, k].rearrange("p (b n) -> p b n", b=2), z[:, k].rearrange(
                            "p (b w n) -> p b w n", b=2, w=2)[:, :, 0, :], ACT.Silu,
                            scale=1.0 / W_SCALE).then_inc(silu_set, 1)
                    return stage

                def act_high(k):
                    def stage(t, p):
                        act.wait_ge(act_set, 2 * t + k + 1)
                        need(act, y_done, t - 1)
                        nc.scalar.activation(act_hi[:, p, 2 * k:2 * k + 2].rearrange("p b n -> p (b n)"),
                                             act_f[:, k], ACT.Copy).then_inc(acthi_set, 1)
                    return stage

                act.wait_ge(ph2, 1)
                nc.scalar.activation(coef[:, 0], gap[:], ACT.Exp, scale=1.0 / W_SCALE).then_inc(coef_e, 1)
                pipeline(act, [(1, silu(0)), (1, silu(1)), (1, act_high(0)), (1, act_high(1))], 2, NX)

                def store(g, p):
                    act.wait_ge(sum2_set, 8 * (g + 1))
                    act.dma_start(out[:, bass.ds(g * 8, 8), :], xall[:, bass.ds(g * 8, 8), :]).then_inc(stored, 16)

                pipeline(act, [(0, store)], 0, 8)
                act.wait_ge(stored, 16 * 8)

            @block.vector
            def _(dve):
                nc.vector.memset(zbias[:], Z_LN).then_inc(zb_set, 1)
                dve.wait_ge(wa_hi_set, 1)
                nc.vector.scalar_tensor_tensor(out=wa_lo[:], in0=wa_f[:], scalar=W_SCALE, in1=wa_hi[:],
                                               op0=ALU.mult, op1=ALU.subtract).then_inc(wa_lo_set, 1)
                dve.wait_ge(rf_hi_set, 1)
                nc.vector.tensor_tensor(out=rf[64:96, :], in0=rf_f[64:96, :], in1=rf[64:96, :],
                                        op=ALU.subtract).then_inc(rf_set, 1)
                dve.wait_ge(pset, 17)

                def stats(b, p, k, mv, nt, st, base):
                    for t in range(2):
                        nc.vector.bn_stats(bn[:, k, t, :], xall[:, bass.ds(b * 2 + t, 1), :].rearrange(
                            "p o d -> p (o d)")).then_inc(st, 1)
                    for t in range(2):
                        wait_apart(dve, dve_passed, st, base + t + 1)
                        nc.vector.bn_aggr(mv[:, p, t, :], bn[:, k, t, :]).then_inc(st, 1)
                    dve.wait_ge(st, base + 4)
                    nc.vector.tensor_scalar(nt[:, p, 0], mv[:, p, :, 1], LN_EPS, None, ALU.add).then_inc(st, 1)

                def ln_1(b, p):
                    dve.wait_ge(xload[p], landed(b, p))
                    base = 18 * b
                    wait_apart(dve, dve_passed, xn_set, 2 * (b - 1))
                    stats(b, p, 0, mv1, nt1, ln1, base)
                    a, y, t_, w = (nt1[:, p, k] for k in range(4))
                    dve.wait_ge(ln1, base + 5)
                    nc.vector.tensor_scalar(y.bitcast(I32), a.bitcast(I32), -0.5, GUESS, ALU.mult,
                                            ALU.add).then_inc(ln1, 1)
                    for k in range(3):
                        dve.wait_ge(ln1, base + 4 * k + 6)
                        nc.vector.tensor_tensor(out=t_, in0=a, in1=y, op=ALU.mult).then_inc(ln1, 1)
                        dve.wait_ge(ln1, base + 4 * k + 7)
                        nc.vector.tensor_tensor(out=w, in0=t_, in1=y, op=ALU.mult).then_inc(ln1, 1)
                        dve.wait_ge(ln1, base + 4 * k + 8)
                        nc.vector.tensor_scalar(t_, w, -0.5, 1.5, ALU.mult, ALU.add).then_inc(ln1, 1)
                        dve.wait_ge(ln1, base + 4 * k + 9)
                        nc.vector.tensor_tensor(out=y, in0=y, in1=t_, op=ALU.mult).then_inc(ln1, 1)
                    dve.wait_ge(ln1, base + 18)
                    need(dve, xnhi_set, b - 1)
                    need(dve, xnlo_set, b - 1)
                    for t in range(2):
                        nc.vector.tensor_scalar(xn_f[:, p, t, :], xall[:, bass.ds(b * 2 + t, 1), :].rearrange(
                            "p o d -> p (o d)"), mv1[:, p, t, 0:1], y[:, t:t + 1], ALU.subtract,
                            ALU.mult).then_inc(xn_set, 1)
                    dve.wait_ge(xnhi_set, b + 1)
                    dve.wait_ge(xn_set, 2 * (b + 1))
                    nc.vector.tensor_tensor(out=xn_s[:, p, 1], in0=xn_f[:, p], in1=xn_s[:, p, 0],
                                            op=ALU.subtract).then_inc(xnlo_set, 1)

                def split(b, p):
                    for t in range(2):
                        dve.wait_ge(v_set, 2 * b + t + 1)
                        e = ext[:, p, t]
                        nc.vector.tensor_tensor(out=e[:, :, 32:64], in0=bQ[:, t, 0:256].rearrange(
                            "p (g c) -> p g c", g=8), in1=e[:, :, 0:32], op=ALU.subtract).then_inc(qlo_set, 1)
                        ins = nc.vector.tensor_tensor(
                            out=vx[:, p, t, 1, :, 0:16], in0=bQ[:, t, 256:384].rearrange("p (j c) -> p j c", j=8),
                            in1=vx[:, p, t, 0, :, 0:16], op=ALU.subtract)
                        if t == 1:
                            ins.then_inc(q_read, 1)
                    e = ext[:, p].rearrange("p t g c -> p (t g) c")
                    nc.vector.tensor_copy(e[:, :, 64:96], e[:, :, 0:32]).then_inc(slab2_set, 1)
                    need(dve, nrm_set, b - 1)
                    nc.vector.tensor_reduce(nrm[:, p, 0], sq[:, p].rearrange("p t (h d) -> p (t h) d", d=HD),
                                            AX.X, ALU.add).then_inc(ss_set, 1)

                def exp_lo(k):
                    def stage(b, p):
                        dve.wait_ge(z_exp, 4 * b + k + 1)
                        if k < 2:
                            src, dst, done = eq[:, p, k], eq_lo[:, p, k], eqlo_set
                            need(dve, o_done, b - 1)
                        else:
                            src, dst, done = ek[:, k - 2], ek_lo[:, k - 2], eklo_set
                            need(dve, kv_done, b)
                        nc.vector.tensor_tensor(out=dst, in0=src, in1=bf_hi(src), op=ALU.subtract).then_inc(done, 1)
                    return stage

                def kv_parts(b, p):
                    dve.wait_ge(kv_done, b + 1)
                    need(dve, o_done, b)
                    need(dve, kv_st, 3 * b)
                    nc.vector.tensor_tensor(out=kvm[:, :, 0:16], in0=m_kv[:, :, 0:16],
                                            in1=kvmask[:, 0:16].unsqueeze(1).to_broadcast([P, 8, 16]), op=ALU.mult)
                    nc.vector.tensor_tensor(out=kvm[:, :, 16:18], in0=m_kv[:, :, 16:17].to_broadcast([P, 8, 2]),
                                            in1=kvmask[:, 16:18].unsqueeze(1).to_broadcast([P, 8, 2]),
                                            op=ALU.mult).then_inc(m_read, 1)
                    dve.wait_ge(m_read, reads_before(BANK_M, M_KV, b) + 1)
                    nc.vector.tensor_copy(kvp[:, 0], kvm[:]).then_inc(kv_st, 1)
                    dve.wait_ge(kv_st, 3 * b + 1)
                    nc.vector.tensor_tensor(out=kvr[:], in0=kvm[:], in1=kvp[:, 0], op=ALU.subtract).then_inc(kv_st, 1)
                    dve.wait_ge(kv_st, 3 * b + 2)
                    nc.vector.tensor_copy(kvp[:, 1], kvr[:]).then_inc(kv_st, 1)
                    dve.wait_ge(kv_st, 3 * b + 3)
                    nc.vector.tensor_tensor(out=kvp[:, 2], in0=kvr[:], in1=kvp[:, 1], op=ALU.subtract).then_inc(kv_set, 1)

                def divide(b, p):
                    need(dve, athi_set, b)
                    need(dve, atlo_set, b)
                    need(dve, at_st, 3 * b)
                    dve.wait_ge(o_done, b + 1)
                    o = m_out.rearrange("p t j c -> p (t j) c")
                    nc.vector.tensor_scalar(den[:], o[:, :, 16:18], 1e-6 * Z2, None, ALU.add).then_inc(at_st, 1)
                    dve.wait_ge(at_st, 3 * b + 1)
                    nc.vector.reciprocal(rden[:], den[:]).then_inc(at_st, 1)
                    dve.wait_ge(at_st, 3 * b + 2)
                    nc.vector.tensor_tensor(
                        out=at_f[:].rearrange("p t (j h c) -> p (t j) h c", j=8, h=2),
                        in0=o[:, :, 0:16].rearrange("p j (h c) -> p j h c", h=2),
                        in1=rden[:].unsqueeze(3).to_broadcast([P, 16, 2, 8]), op=ALU.mult).then_inc(at_st, 1)
                    dve.wait_ge(at_st, 3 * (b + 1))
                    nc.vector.tensor_copy(free[:], at_f[:, 0, 0:1]).then_inc(m_read, 1)
                    dve.wait_ge(athi_set, b + 1)
                    dve.wait_ge(at_st, 3 * (b + 1))
                    nc.vector.tensor_tensor(out=at_s[:, 1], in0=at_f[:], in1=at_s[:, 0],
                                            op=ALU.subtract).then_inc(atlo_set, 1)

                def residual(b, p):
                    dve.wait_ge(bias_set, b + 1)
                    dve.wait_ge(w_done, b + 1)
                    for t in range(2):
                        v = xall[:, bass.ds(b * 2 + t, 1), :].rearrange("p o d -> p (o d)")
                        nc.vector.scalar_tensor_tensor(out=v, in0=bQ[:, t, 384:512], scalar=1.0 / (W_SCALE * W_SCALE),
                                                       in1=v, op0=ALU.mult, op1=ALU.add).then_inc(x1_set, 1)
                    dve.wait_ge(x1_set, 2 * (b + 1))
                    nc.vector.tensor_copy(free[:], at_f[:, 0, 0:1]).then_inc(q_read, 1)
                    need(dve, x2_set, 2 * (b - 1))
                    wait_apart(dve, dve_passed, ln2_set, 13 * (b - 1))
                    stats(b, p, 1, mv2, nt2, ln2_st, 5 * b)

                def ln_2(b, p):
                    dve.wait_ge(ln2_set, 13 * (b + 1))
                    need(dve, x2hi_set, b)
                    need(dve, x2lo_set, b)
                    for t in range(2):
                        nc.vector.tensor_scalar(x2_f[:, t, :], xall[:, bass.ds(b * 2 + t, 1), :].rearrange(
                            "p o d -> p (o d)"), mv2[:, p, t, 0:1], nt2[:, p, 1, t:t + 1], ALU.subtract,
                            ALU.mult).then_inc(x2_set, 1)
                    dve.wait_ge(x2hi_set, b + 1)
                    dve.wait_ge(x2_set, 2 * (b + 1))
                    nc.vector.tensor_tensor(out=rows[:, p, 0, :, D:2 * D], in0=x2_f[:], in1=rows[:, p, 0, :, 0:D],
                                            op=ALU.subtract).then_inc(x2lo_set, 1)
                    dve.wait_ge(x2lo_set, b + 1)
                    nc.vector.tensor_copy(rows[:, p, 1, :, 0:2 * D], rows[:, p, 0, :, 0:2 * D]).then_inc(rows_set, 1)
                    for k in range(TOPK):
                        nc.vector.tensor_copy(rows[:, p, k, :, ID:ID + 2].bitcast(I32),
                                              ids[:, k, bass.ds(b * 2, 2)].unsqueeze(2)).then_inc(rows_set, 1)

                def route_a(b, p):
                    n = 14 * b
                    bc = lambda a: a.unsqueeze(2).to_broadcast([P, 2, E])
                    rk = rank[:].unsqueeze(1).to_broadcast([P, 2, E])
                    dve.wait_ge(rt_done, b + 1)
                    need(dve, rt_st, n)
                    nc.vector.tensor_copy(lg[:], m_rt).then_inc(m_read, 1)
                    dve.wait_ge(m_read, reads_before(BANK_M, M_RT, b) + 1)
                    src = lg
                    for k in range(2):
                        nc.vector.tensor_reduce(top[:, k], src[:], AX.X, ALU.max).then_inc(rt_st, 1)
                        dve.wait_ge(rt_st, n + 6 * k + 1)
                        nc.vector.tensor_tensor(out=cand[:, k, 0], in0=src[:], in1=bc(top[:, k]),
                                                op=ALU.is_equal).then_inc(rt_st, 1)
                        dve.wait_ge(rt_st, n + 6 * k + 2)
                        nc.vector.tensor_tensor(out=cand[:, k, 1], in0=cand[:, k, 0], in1=rk, op=ALU.mult).then_inc(rt_st, 1)
                        dve.wait_ge(rt_st, n + 6 * k + 3)
                        nc.vector.tensor_reduce(top[:, 2 + k], cand[:, k, 1], AX.X, ALU.max).then_inc(rt_st, 1)
                        dve.wait_ge(rt_st, n + 6 * k + 4)
                        nc.vector.tensor_tensor(out=pick[:, k], in0=cand[:, k, 1], in1=bc(top[:, 2 + k]),
                                                op=ALU.is_equal).then_inc(rt_st, 1)
                        dve.wait_ge(rt_st, n + 6 * k + 5)
                        if k == 0:
                            nc.vector.scalar_tensor_tensor(out=lg2[:], in0=pick[:, 0], scalar=-3.0e38, in1=lg[:],
                                                           op0=ALU.mult, op1=ALU.add).then_inc(rt_st, 1)
                            dve.wait_ge(rt_st, n + 6)
                            src = lg2
                    nc.vector.tensor_tensor(out=gap[:, bass.ds(b * 2, 2)], in0=top[:, 1], in1=top[:, 0],
                                            op=ALU.subtract).then_inc(rt_st, 1)
                    need(dve, pos_done, b - 1)
                    nc.vector.tensor_tensor(out=both[:, p], in0=pick[:, 0], in1=pick[:, 1],
                                            op=ALU.add).then_inc(both_set, 1)

                def route_b(b, p):
                    dve.wait_ge(pos_done, b + 1)
                    nc.vector.tensor_tensor(out=where[:], in0=m_pos, in1=ebase[:].unsqueeze(1).to_broadcast([P, 2, E]),
                                            op=ALU.add).then_inc(m_read, 1)
                    nc.vector.tensor_tensor(out=cum1[:], in0=mcum[:], in1=both[:, p, 0], op=ALU.add).then_inc(cum_st, 1)
                    dve.wait_ge(m_read, reads_before(BANK_M, M_POS, b) + 1)
                    for k in range(TOPK):
                        ins = nc.vector.tensor_tensor(out=hit[:, k], in0=pick[:, k], in1=where[:], op=ALU.mult)
                    ins.then_inc(rt_st, 1)
                    dve.wait_ge(cum_st, b + 1)
                    nc.vector.tensor_tensor(out=mcum[:], in0=cum1[:], in1=both[:, p, 1], op=ALU.add).then_inc(cum_set, 1)
                    dve.wait_ge(rt_st, 14 * b + 13)
                    nc.vector.tensor_reduce(slot_f[:], hit[:].rearrange("p k t e -> p (k t) e"), AX.X,
                                            ALU.add).then_inc(rt_st, 1)
                    dve.wait_ge(rt_st, 14 * b + 14)
                    need(dve, scat[p], 32 * (b - p))
                    nc.vector.tensor_copy(slot[:, p], slot_f[:]).then_inc(slot_set, 1)

                def w_part(b, p):
                    dve.wait_ge(wsplit_hi, b + 1)
                    w = bass.ds(b * WCH, WCH)
                    nc.vector.scalar_tensor_tensor(out=w_lo[:, w], in0=w_st[:, p, :], scalar=W_SCALE, in1=w_hi[:, w],
                                                   op0=ALU.mult, op1=ALU.subtract).then_inc(wsplit_lo, 1)

                pipeline(dve, [(4, ln_2), (0, ln_1), (3, divide), (4, route_a), (3, residual), (2, exp_lo(2)),
                               (2, exp_lo(3)), (1, split), (2, kv_parts), (4, route_b), (2, exp_lo(0)),
                               (2, exp_lo(1)), (0, w_part)])

                n = [0]

                def chain(ins):
                    n[0] += 1
                    ins.then_inc(ph2, 1)
                    dve.wait_ge(ph2, n[0])

                dve.wait_ge(cnt_done, 1)
                chain(nc.vector.tensor_copy(cnt[:], bM[:, 0:E]))
                nc.vector.tensor_copy(cnt_i[:], cnt[:]).then_inc(cnt_set, 1)
                chain(nc.vector.tensor_scalar(up_i[:, 0], cnt[:], float(SLOTS - 1), None, ALU.add))
                chain(nc.vector.tensor_scalar(up_i[:, 1], up_i[:, 0], SLOTS.bit_length() - 1, None,
                                              ALU.logical_shift_right))
                chain(nc.vector.tensor_copy(ntile[:], up_i[:, 1]))
                chain(nc.vector.tensor_copy(ends[:, 0:1], ntile[:, 0:1]))
                for e in range(1, E):
                    chain(nc.vector.tensor_tensor(out=ends[:, e:e + 1], in0=ends[:, e - 1:e], in1=ntile[:, e:e + 1],
                                                  op=ALU.add))
                chain(nc.vector.tensor_scalar(skip[:], ntile[:], -float(SLOTS), float(CAP), ALU.mult, ALU.add))
                chain(nc.vector.tensor_tensor(out=past[:], in0=tnum[:].unsqueeze(2).to_broadcast([P, NX, E]),
                                              in1=ends[:].unsqueeze(1).to_broadcast([P, NX, E]), op=ALU.is_ge))
                chain(nc.vector.tensor_tensor(out=jump[:], in0=past[:], in1=skip[:].unsqueeze(1).to_broadcast(
                    [P, NX, E]), op=ALU.mult))
                chain(nc.vector.tensor_reduce(tab_f[:, 0, 0], past[:], AX.X, ALU.add))
                chain(nc.vector.tensor_reduce(tab_f[:, 0, 1], jump[:], AX.X, ALU.add))
                chain(nc.vector.scalar_tensor_tensor(out=tab_f[:, 1, 1], in0=tnum[:], scalar=float(SLOTS),
                                                     in1=tab_f[:, 0, 1], op0=ALU.mult, op1=ALU.add))
                chain(nc.vector.tensor_scalar(tab[:, 0], tab_f[:, 0, 0], float(E - 1), None, ALU.min))
                nc.vector.tensor_scalar(tab[:, 1], tab_f[:, 1, 1], float(E * CAP), None, ALU.min).then_inc(tab_set, 1)
                dve.wait_ge(coef_e, 1)
                chain(nc.vector.tensor_scalar(coef[:, 1], coef[:, 0], 1.0, None, ALU.add))
                chain(nc.vector.reciprocal(coef[:, 2], coef[:, 1]))
                nc.vector.tensor_tensor(out=coef[:, 3], in0=coef[:, 0], in1=coef[:, 2], op=ALU.mult).then_inc(coef_set, 1)

                def xl_copy(t, p):
                    dve.wait_ge(xl_turned, t + 1)
                    need(dve, h_done, 2 * (t - 1))
                    nc.vector.tensor_copy(xlT[:, p].rearrange("p a n -> p (a n)"), bT[:, 0:512]).then_inc(xlT_set, 1)
                    dve.wait_ge(xl_load[p], 8 * (t - p) + 16)
                    nc.vector.tensor_copy(row_id[:, bass.ds(t, 1), :].unsqueeze(3),
                                          xl[:, p, :, ID:ID + 2].bitcast(I32).unsqueeze(1)).then_inc(id_kept, 1)

                def gated(k):
                    def stage(t, p):
                        dve.wait_ge(silu_set, 2 * t + k + 1)
                        need(dve, acthi_set, 2 * t + k - 1)
                        need(dve, actlo_set, 2 * t + k - 1)
                        nc.vector.tensor_tensor(out=act_f[:, k].rearrange("p (b n) -> p b n", b=2),
                                                in0=z[:, k].rearrange("p (b w n) -> p b w n", b=2, w=2)[:, :, 1, :],
                                                in1=gate[:, k].rearrange("p (b n) -> p b n", b=2),
                                                op=ALU.mult).then_inc(act_set, 1)
                    return stage

                def act_low(k):
                    def stage(t, p):
                        dve.wait_ge(acthi_set, 2 * t + k + 1)
                        nc.vector.tensor_tensor(
                            out=act_lo[:, p, 2 * k:2 * k + 2].rearrange("p b n -> p (b n)"), in0=act_f[:, k],
                            in1=act_hi[:, p, 2 * k:2 * k + 2].rearrange("p b n -> p (b n)"),
                            op=ALU.subtract).then_inc(actlo_set, 1)
                    return stage

                def y_copy(t, p):
                    dve.wait_ge(y_done, t + 1)
                    need(dve, y_scat[p], 16 * (t - p))
                    nc.vector.tensor_scalar(y[:, p].rearrange("p h d -> p (h d)"), bQ[:, p, 0:256],
                                            1.0 / (W_SCALE * W_SCALE), None, ALU.mult).then_inc(y_set, 1)
                    dve.wait_ge(id_kept, t + 1)
                    nc.vector.tensor_copy(put_id[:, p, :].unsqueeze(1), row_id[:, bass.ds(t, 1), :]).then_inc(y_set, 1)

                pipeline(dve, [(1, gated(0)), (0, xl_copy), (1, gated(1)), (1, act_low(0)), (1, act_low(1)),
                               (2, y_copy)], 2, NX)

                def combine(g, p):
                    dve.wait_ge(pl_load[p], 16 * (g - p) + 32)
                    for k, done in ((0, sum1_set), (1, sum2_set)):
                        if k:
                            dve.wait_ge(sum1_set, 8 * (g + 1))
                        for t in range(8):
                            v = xall[:, bass.ds(g * 8 + t, 1), :].rearrange("p o d -> p (o d)")
                            nc.vector.scalar_tensor_tensor(
                                out=v, in0=pl[:, p, k, t, :], scalar=coef[:, 2 + k, bass.ds(g * 8 + t, 1)], in1=v,
                                op0=ALU.mult, op1=ALU.add).then_inc(done, 1)

                dve.wait_ge(coef_set, 1)
                pipeline(dve, [(0, combine)], 0, 8)

            @block.tensor
            def _(pe):
                mm = nc.tensor.matmul
                pe.wait_ge(pset, 17)
                pe.wait_ge(wa_lo_set, 1)
                pe.wait_ge(rf_set, 1)

                def free_bank(s, bank, k, b):
                    need(pe, s, reads_before(bank, k, b))

                def three(out_, hi, lo, w_h, w_l, start):
                    mm(out_, hi, w_h, start=start, stop=False, skip_group_check=True)
                    mm(out_, hi, w_l, start=False, stop=False, skip_group_check=True)
                    return mm(out_, lo, w_h, start=False, stop=True, skip_group_check=True)

                def turn(src, n):
                    for k in range(n):
                        last = nc.tensor.transpose(bT[:, P * k:P * k + P], src(k), ident[:])
                    return last

                def ext_turn(half, k, done):
                    def stage(b, p):
                        pe.wait_ge(nrm_set, b + 1)
                        pe.wait_ge(slab2_set, b + 1)
                        free_bank(t_read, BANK_T, k, b)
                        turn(lambda n: ext[:, p, n % 2, 4 * half + n // 2, :], 8).then_inc(done, 1)
                    return stage

                def ln1_turn(b, p):
                    pe.wait_ge(xnlo_set, b + 1)
                    free_bank(t_read, BANK_T, T_LN1, b)
                    turn(lambda n: xn_s[:, p, n // 2, n % 2, :], 4).then_inc(t_ln1, 1)

                def att_turn(b, p):
                    pe.wait_ge(atlo_set, b + 1)
                    free_bank(t_read, BANK_T, T_ATT, b)
                    turn(lambda n: at_s[:, n // 2, n % 2, :], 4).then_inc(t_att, 1)

                def ln2_turn(b, p):
                    pe.wait_ge(x2lo_set, b + 1)
                    free_bank(t_read, BANK_T, T_LN2, b)
                    turn(lambda n: rows[:, p, 0, n % 2, D * (n // 2):D * (n // 2) + D], 4).then_inc(t_ln2, 1)

                def qkv(b, p):
                    pe.wait_ge(t_read, reads_before(BANK_T, T_LN1, b) + 1)
                    free_bank(q_read, BANK_Q, Q_QKV, b)
                    for t in range(2):
                        c = slice(P * t, P * t + P)
                        three(bQ[:, t, 0:384], xT[:, p, 0, c], xT[:, p, 1, c], wa_hi[:, 0:384], wa_lo[:, 0:384],
                              True).then_inc(q_done, 1)

                def features(k):
                    def stage(b, p):
                        pe.wait_ge(t_read, reads_before(BANK_T, T_EXTQ if k < 2 else T_EXTK, b) + 1)
                        need(pe, z_exp, 4 * b + k - 1)
                        for n in range(4):
                            o = z[:, k % 2, 256 * n:256 * n + 256]
                            if k < 2:
                                last = mm(o, rf[:, P * (n % 2):P * (n % 2) + P], extT[:, p, 2 * k + n // 2, :],
                                          start=True, stop=True, skip_group_check=True)
                            else:
                                last = mm(o, extT[:, p, 4 + n, P * (k - 2):P * (k - 1)], rf[:], start=True, stop=True,
                                          skip_group_check=True)
                        last.then_inc(z_done, 1)
                    return stage

                def kv(b, p):
                    free_bank(m_read, BANK_M, M_KV, b)
                    pe.wait_ge(q_read, reads_before(BANK_Q, Q_QKV, b) + 1)
                    for t in range(2):
                        pe.wait_ge(eklo_set, 2 * b + t + 1)
                        for j in range(8):
                            f = slice(P * j, P * j + P)
                            for e, c in ((bf_hi(ek[:, t, f]), 0), (bf_hi(ek[:, t, f]), 1), (ek_lo[:, t, f], 0),
                                         (ek_lo[:, t, f], 1)):
                                first = t == 0 and j == 0 and c == 0 and e.dtype == BF16
                                last = mm(m_kv[:, j, :], e, vx[:, p, t, c, j, :], start=first, stop=False,
                                          skip_group_check=True)
                    last.then_inc(kv_done, 1)

                def attend(b, p):
                    free_bank(m_read, BANK_M, M_OUT, b)
                    pe.wait_ge(kv_set, b + 1)
                    pe.wait_ge(eqlo_set, 2 * (b + 1))
                    for t in range(2):
                        for j in range(8):
                            f = slice(256 * (j % 4) + P * t, 256 * (j % 4) + P * t + P)
                            n = 0
                            for e in (bf_hi(eq[:, p, j // 4, f]), eq_lo[:, p, j // 4, f]):
                                for c in range(3):
                                    last = mm(m_out[:, t, j, :], e, kvp[:, c, j, :], start=(t + j + n == 0),
                                              stop=False, skip_group_check=True)
                                    n += 1
                    last.then_inc(o_done, 1)

                def w_out(b, p):
                    pe.wait_ge(t_read, reads_before(BANK_T, T_ATT, b) + 1)
                    free_bank(q_read, BANK_Q, Q_WOUT, b)
                    for t in range(2):
                        c = slice(P * t, P * t + P)
                        last = three(bQ[:, t, 384:512], atT[:, 0, c], atT[:, 1, c], wa_hi[:, 384:512],
                                     wa_lo[:, 384:512], True)
                    last.then_inc(w_done, 1)

                def router(b, p):
                    pe.wait_ge(t_read, reads_before(BANK_T, T_LN2, b) + 1)
                    free_bank(m_read, BANK_M, M_RT, b)
                    for t in range(2):
                        c = slice(P * t, P * t + P)
                        last = three(m_rt[:, t, :], x2T[:, 0, c], x2T[:, 1, c], wa_hi[:, 512:520], wa_lo[:, 512:520],
                                     t == 0)
                    last.then_inc(rt_done, 1)

                def positions(b, p):
                    pe.wait_ge(both_set, b + 1)
                    need(pe, cum_set, b)
                    free_bank(m_read, BANK_M, M_POS, b)
                    mm(m_pos[:, 0, :], tri[:], both[:, p, 0, :], start=True, stop=False, skip_group_check=True)
                    mm(m_pos[:, 0, :], ones[:], mcum[:], start=False, stop=True, skip_group_check=True)
                    mm(m_pos[:, 1, :], tri[:], both[:, p, 1, :], start=False, stop=False, skip_group_check=True)
                    mm(m_pos[:, 1, :], ones[:], mcum[:], start=False, stop=False, skip_group_check=True)
                    mm(m_pos[:, 1, :], ones[:], both[:, p, 0, :], start=False, stop=True,
                       skip_group_check=True).then_inc(pos_done, 1)

                pipeline(pe, [(2, ext_turn(0, T_EXTQ, t_extq)), (2, ext_turn(1, T_EXTK, t_extk)), (3, attend),
                              (2, features(0)), (0, ln1_turn), (2, features(1)), (3, att_turn), (4, ln2_turn),
                              (2, features(2)), (4, router), (3, w_out), (2, features(3)), (1, qkv), (2, kv),
                              (4, positions)])

                pe.wait_ge(cum_set, NB)
                need(pe, m_read, reads_before(BANK_M, M_OUT, NB + LAG))
                mm(bM[:, 0:E], ones[:], mcum[:], start=True, stop=True, skip_group_check=True).then_inc(cnt_done, 1)

                w_h = w_hi[:].rearrange("p (e w n) -> p e w n", e=E, w=3)
                w_l = w_lo[:].rearrange("p (e w n) -> p e w n", e=E, w=3)
                expert = {}

                def rows_turn(t, p):
                    pe.wait_ge(xl_load[p], 8 * (t - p) + 16)
                    need(pe, xlT_set, t)
                    turn(lambda n: xl[:, p, n % 2, D * (n // 2):D * (n // 2) + D], 4).then_inc(xl_turned, 1)

                def load_expert(t):
                    return nc.values_load(tab[0:1, 0, bass.ds(t, 1)], engines=[mybir.EngineType.PE], min_val=0,
                                          max_val=E - 1, skip_runtime_bounds_check_because="clamped to the last expert")

                def hidden(k):
                    def stage(t, p):
                        if k == 0:
                            expert[1] = load_expert(t)
                            pe.wait_ge(xlT_set, t + 1)
                        e = expert[1]
                        need(pe, act_set, 2 * t + k - 1)
                        for b in range(2):
                            for w in range(2):
                                c = slice(256 * k + P * b, 256 * k + P * b + P)
                                o = z[:, k, 512 * b + 256 * w:512 * b + 256 * w + 256]
                                mm(o, w_h[:, bass.ds(e, 1), w, c].rearrange("p o n -> p (o n)"), xlT[:, p, 0, :],
                                   start=(w == 0), stop=False, skip_group_check=True)
                                mm(o, w_h[:, bass.ds(e, 1), w, c].rearrange("p o n -> p (o n)"), xlT[:, p, 1, :],
                                   start=False, stop=False, skip_group_check=True)
                                last = mm(o, w_l[:, bass.ds(e, 1), w, c].rearrange("p o n -> p (o n)"),
                                          xlT[:, p, 0, :], start=False, stop=True, skip_group_check=True)
                        last.then_inc(h_done, 1)
                    return stage

                def output(t, p):
                    e = load_expert(t)
                    pe.wait_ge(actlo_set, 2 * (t + 1))
                    need(pe, y_set, 2 * (t - 1))
                    for h in range(2):
                        o = bQ[:, p, P * h:P * h + P]
                        c = slice(P * h, P * h + P)
                        for b in range(4):
                            w = slice(P * b, P * b + P)
                            w2h = w_h[:, bass.ds(e, 1), 2, w].rearrange("p o n -> p (o n)")
                            w2l = w_l[:, bass.ds(e, 1), 2, w].rearrange("p o n -> p (o n)")
                            mm(o, act_hi[:, p, b, c], w2h, start=(h + b == 0), stop=False, skip_group_check=True)
                            mm(o, act_hi[:, p, b, c], w2l, start=False, stop=False, skip_group_check=True)
                            last = mm(o, act_lo[:, p, b, c], w2h, start=False, stop=True, skip_group_check=True)
                    last.then_inc(y_done, 1)

                pe.wait_ge(tab_set, 1)
                pe.wait_ge(wsplit_lo, NB)
                need(pe, z_exp, 4 * NB)
                need(pe, t_read, reads_before(BANK_T, T_EXTQ, NB + LAG))
                need(pe, q_read, 2 * NB)
                pipeline(pe, [(0, rows_turn), (1, hidden(0)), (1, hidden(1)), (2, output)], 2, NX)


def kernel(L0_attn_x, L0_attn_w_qkv, L0_attn_w_out, L0_attn_b_out, L0_attn_random_features, L0_ffn_gate_w, L0_ffn_w1,
           L0_ffn_w3, L0_ffn_w2):
    import numpy as np
    import concourse.bacc as bacc
    from concourse.bass_utils import run_bass_kernel_spmd

    cont = np.ascontiguousarray
    wa = np.concatenate([np.asarray(w).T for w in (L0_attn_w_qkv, L0_attn_w_out, L0_ffn_gate_w)], axis=1)
    w13 = [np.asarray(w).transpose(2, 0, 1) for w in (L0_ffn_w1, L0_ffn_w3)]
    w2 = np.asarray(L0_ffn_w2).transpose(2, 0, 1).reshape(4, P, E, D).transpose(1, 2, 0, 3).reshape(P, E, 4 * D)
    rfc = np.zeros((P, 4 * F), np.float32)
    for h in range(4):
        for part in range(2):
            rfc[96 + 4 * part + h, F * h:F * h + F] = -8.0
    mask = np.zeros((P, 18), np.float32)
    for r in range(P):
        mask[r, HD * (r // F):HD * (r // F) + HD] = 1.0
        mask[r, 16 + r // F] = 1.0
    arrays = {
        "x": cont(np.asarray(L0_attn_x).reshape(T, D)),
        "wa": cont(wa),
        "bout": cont(np.broadcast_to(np.asarray(L0_attn_b_out), (P, D))),
        "rft": cont(np.asarray(L0_attn_random_features).T),
        "rfc": rfc,
        "wffn": cont(np.concatenate([*w13, w2], axis=2).reshape(P, E * 3 * HID)),
        "mask": mask,
    }
    nc = bacc.Bacc("TRN2", target_bir_lowering=False, num_devices=1)
    ins = {n: nc.dram_tensor(n, a.shape, F32, kind="ExternalInput").ap() for n, a in arrays.items()}
    out = nc.dram_tensor("out", (T, D), F32, kind="ExternalOutput").ap()
    xs = nc.dram_tensor("xs", (E * CAP + SLOTS, ROW), F16, kind="Internal").ap()
    planes = nc.dram_tensor("planes", (TOPK * T, D), F32, kind="Internal").ap()
    ins["x"] = ins["x"].rearrange("(t p) d -> p t d", p=P)
    out = out.rearrange("(t p) d -> p t d", p=P)
    build(nc, **ins, out=out, xs=xs, planes=planes)
    r = run_bass_kernel_spmd(nc, [arrays], core_ids=[0])
    return r.results[0]["out"].reshape(L0_attn_x.shape)
```

```python
from contextlib import ExitStack

import concourse.bass as bass
from concourse import mybir

F32, F16, BF16 = mybir.dt.float32, mybir.dt.float16, mybir.dt.bfloat16
I32, U32 = mybir.dt.int32, mybir.dt.uint32
ACT, ALU, AX = mybir.ActivationFunctionType, mybir.AluOpType, mybir.AxisListType

P = 128
T = 8192
D = 128
H, HD, F = 16, 8, 64
NT = T // P
NB = 32
E, HID, TOPK = 8, 512, 2
SLOTS = 256
NX = T * TOPK // SLOTS + E
CAP = T + SLOTS
ROW = 264
ID, ODDS = 256, 258
PAD_ID = T
W_SCALE = 16.0
Z_LN = 8 * 0.6931471805599453
Z2 = 65536.0
LN_EPS = 1e-5
WCH = E * 3 * HID // NB
LAG = 5
RS = 11
GUESS = float(0x5F3759DF)
R_LN1, R_NORM, R_LN2 = 1, 2, 4


def need(eng, sem, value):
    if isinstance(value, int) and value <= 0:
        return
    eng.wait_ge(sem, value)


def wait_apart(eng, passed, sem, value):
    if isinstance(value, int):
        return need(eng, sem, value)
    eng.wait_ge(sem, value).then_inc(passed, 1)


def pipeline(eng, stages, last=LAG, n=NB):
    last += last % 2

    def iterate(it):
        for lag, stage in stages:
            if lag is None:
                stage(it, it % 2)
            elif 0 <= it - lag < n:
                stage(it - lag, (it - lag) % 2)

    for it in range(last + 2):
        iterate(it)
    with eng.Fori(last // 2 + 1, n // 2) as i:
        for u in range(2):
            for lag, stage in stages:
                lag = lag or 0
                stage(i * 2 + (u - lag), (u - lag) % 2)
    for it in range(n, n + last):
        iterate(it)


def batches(it, lag):
    return max(0, min(it - lag + 1, NB)) if isinstance(it, int) else it - lag + 1


def reads_before(uses, k, b):
    it = b + uses[k][0]
    if isinstance(b, int):
        return sum(n * min(max(it - lag + (j < k), 0), NB) for j, (lag, n) in enumerate(uses))
    return it * sum(n for _, n in uses) + sum(n * ((j < k) - lag) for j, (lag, n) in enumerate(uses))


BANK_T = [(2, 1), (4, 1), (2, 1), (3, 1), (1, 1)]
T_EXTQ, T_LN2, T_EXTK, T_ATT, T_LN1 = range(5)
BANK_Q = [(3, 1), (1, 1)]
Q_WOUT, Q_QKV = range(2)
BANK_M = [(3, 1), (4, 1), (2, 1), (4, 1)]
M_OUT, M_RT, M_KV, M_POS = range(4)


def build(nc, x, wa, bout, rft, rfc, wffn, mask, out, xs):
    with ExitStack() as ctx:
        def sb(name, shape, dt):
            return ctx.enter_context(nc.sbuf_tensor(name, shape, dt))

        def psum(name, shape, dt):
            return ctx.enter_context(nc.psum_tensor(name, shape, dt))

        def sem(name):
            return ctx.enter_context(nc.semaphore(name))

        ident = sb("ident", [P, P], F16)
        tri = sb("tri", [P, P], F16)
        ones = sb("ones", [P, P], F16)
        wa_f = sb("wa_f", [P, 520], F32)
        wa_hi = sb("wa_hi", [P, 520], F16)
        wa_lo = sb("wa_lo", [P, 520], F16)
        rf_f = sb("rf_f", [P, 4 * F], F32)
        rf = sb("rf", [P, 4 * F], F16)
        b_bc = sb("b_bc", [P, D], F32)
        kvmask = sb("kvmask", [P, 18], F32)
        rank = sb("rank", [P, E], F32)
        ebase = sb("ebase", [P, E], F32)
        ids = sb("ids", [P, NT], I32)
        w_st = sb("w_st", [P, 2, WCH], F32)
        w_hi = sb("w_hi", [P, E * 3 * HID], F16)
        w_lo = sb("w_lo", [P, E * 3 * HID], F16)

        xall = sb("xall", [P, NT, D], F32)
        mcum = sb("mcum", [P, E], F16)

        bn = sb("bn", [P, 2, 2, 6], F32)
        mv1 = sb("mv1", [P, 2, 2, 2], F32)
        rs = sb("rs", [P, 2, 5, 68], F32)
        xn_f = sb("xn_f", [P, 2, 2, D], F32)
        xn_s = sb("xn_s", [P, 2, 2, 2, D], F16)
        xT = sb("xT", [P, 2, 2, 256], F16)
        ext = sb("ext", [P, 2, 2, 8, P], F16)
        sq = sb("sq", [P, 2, 2, 256], F32)
        vx = sb("vx", [P, 2, 2, 2, 8, 17], F16)
        extT = sb("extT", [P, 2, 8, 256], F16)
        eq = sb("eq", [P, 2, 2, 1024], F32)
        eq_lo = sb("eq_lo", [P, 2, 2, 1024], F16)
        ek = sb("ek", [P, 2, 1024], F32)
        ek_lo = sb("ek_lo", [P, 2, 1024], F16)
        kvm = sb("kvm", [P, 8, 18], F32)
        kvr = sb("kvr", [P, 8, 18], F32)
        kvp = sb("kvp", [P, 3, 8, 18], BF16)
        den = sb("den", [P, 16, 2], F32)
        rden = sb("rden", [P, 16, 2], F32)
        at_f = sb("at_f", [P, 2, D], F32)
        at_s = sb("at_s", [P, 2, 2, D], F16)
        atT = sb("atT", [P, 2, 256], F16)
        mv2 = sb("mv2", [P, 2, 2, 2], F32)
        x2_f = sb("x2_f", [P, 2, D], F32)
        rows = sb("rows", [P, 2, TOPK, 2, ROW], F16)
        x2T = sb("x2T", [P, 2, 256], F16)
        lg = sb("lg", [P, 2, E], F32)
        lg2 = sb("lg2", [P, 2, E], F32)
        cand = sb("cand", [P, 2, 2, 2, E], F32)
        top = sb("top", [P, 4, 2], F32)
        pick = sb("pick", [P, 2, 2, E], F32)
        both = sb("both", [P, 2, 2, E], F16)
        gap = sb("gap", [P, 2, 2], F32)
        cum1 = sb("cum1", [P, E], F16)
        zbias = sb("zbias", [P, 1], F32)
        where = sb("where", [P, 2, E], F32)
        hit = sb("hit", [P, 2, 2, E], F32)
        slot_f = sb("slot_f", [P, 4], F32)
        slot = sb("slot", [P, 2, 4], U32)

        pad = sb("pad", [P, 2, ROW], F16)
        cnt = sb("cnt", [P, E], F32)
        cnt_i = sb("cnt_i", [P, E], I32)
        up_i = sb("up_i", [P, 2, E], I32)
        ntile = sb("ntile", [P, E], F32)
        ends = sb("ends", [P, E], F32)
        skip = sb("skip", [P, E], F32)
        tnum = sb("tnum", [P, NX], F32)
        past = sb("past", [P, NX, E], F32)
        jump = sb("jump", [P, NX, E], F32)
        tab_f = sb("tab_f", [P, 2, 2, NX], F32)
        tab = sb("tab", [P, 2, NX], I32)

        xl = sb("xl", [P, 2, 2, ROW], F16)
        xlT = sb("xlT", [P, 2, 2, SLOTS], F16)
        gate = sb("gate", [P, 2, 512], F32)
        act_f = sb("act_f", [P, 2, 512], F32)
        act_hi = sb("act_hi", [P, 2, 4, SLOTS], F16)
        act_lo = sb("act_lo", [P, 2, 4, SLOTS], F16)
        y = sb("y", [P, 2, 2, D], F32)
        row_id = sb("row_id", [P, NX, 2], I32)
        odds1 = sb("odds1", [P, NX, 2], F32)
        coef = sb("coef", [P, NX, 2], F32)
        put_id = sb("put_id", [P, 2, 2], I32)

        z = psum("z", [P, 2, 1024], F32)
        bT = psum("bT", [P, 1024], F16)
        bQ = psum("bQ", [P, 2, 512], F32)
        bM = psum("bM", [P, 512], F32)
        m_out = bM[:, 0:288].rearrange("p (t j c) -> p t j c", t=2, j=8)
        m_kv = bM[:, 288:424].rearrange("p (j c) -> p j c", j=8)
        m_rt = bM[:, 424:440].rearrange("p (t e) -> p t e", t=2)
        m_pos = bM[:, 440:456].rearrange("p (t e) -> p t e", t=2)

        dve_passed, pool_passed = sem("dve_passed"), sem("pool_passed")
        xload = [sem(f"xload{i}") for i in range(2)]
        wload = [sem(f"wload{i}") for i in range(2)]
        cload = sem("cload")
        rload = sem("rload")
        pset = sem("pset")
        wa_hi_set, wa_lo_set, rf_hi_set, rf_set = sem("wa_hi_set"), sem("wa_lo_set"), sem("rf_hi_set"), sem("rf_set")
        wsplit_hi, wsplit_lo = sem("wsplit_hi"), sem("wsplit_lo")
        ln1_st, rs_st = sem("ln1_st"), sem("rs_st")
        xn_set, xnhi_set, xnlo_set, bias_set = sem("xn_set"), sem("xnhi_set"), sem("xnlo_set"), sem("bias_set")
        t_ln1, t_extq, t_extk, t_att, t_ln2 = (sem(n) for n in ("t_ln1", "t_extq", "t_extk", "t_att", "t_ln2"))
        t_read = sem("t_read")
        q_done, q_read, qhi_set, qlo_set, slab2_set, sq_set, ss_set = (
            sem(n) for n in ("q_done", "q_read", "qhi_set", "qlo_set", "slab2_set", "sq_set", "ss_set"))
        v_set, nrm_st, nrm_set = sem("v_set"), sem("nrm_st"), sem("nrm_set")
        z_done, z_exp, eklo_set = sem("z_done"), sem("z_exp"), sem("eklo_set")
        eqlo_set = [sem(f"eqlo_set{i}") for i in range(2)]
        kv_done, kv_st, kv_set = sem("kv_done"), sem("kv_st"), sem("kv_set")
        m_read = sem("m_read")
        o_done, at_st, athi_set, atlo_set = sem("o_done"), sem("at_st"), sem("athi_set"), sem("atlo_set")
        w_done, ln2_st = sem("w_done"), sem("ln2_st")
        x2_set, x2hi_set, x2lo_set, rows_set = sem("x2_set"), sem("x2hi_set"), sem("x2lo_set"), sem("rows_set")
        rt_done, rt_st, both_set, pos_done, slot_set = (
            sem(n) for n in ("rt_done", "rt_st", "both_set", "pos_done", "slot_set"))
        cum_set, cum_st, zb_set = sem("cum_set"), sem("cum_st"), sem("zb_set")
        scat = [sem(f"scat{i}") for i in range(2)]

        cnt_done, ph2, cnt_set, tab_set, tail = (
            sem(n) for n in ("cnt_done", "ph2", "cnt_set", "tab_set", "tail"))
        xl_load = [sem(f"xl_load{i}") for i in range(2)]
        y_scat = [sem(f"y_scat{i}") for i in range(2)]
        id_kept = sem("id_kept")
        xl_turned, xlT_set, h_done, silu_set, act_set, acthi_set, actlo_set, y_done, y_set = (
            sem(n) for n in ("xl_turned", "xlT_set", "h_done", "silu_set", "act_set", "acthi_set", "actlo_set",
                             "y_done", "y_set"))
        odds_set, odds1_set, coef_set, stored = sem("odds_set"), sem("odds1_set"), sem("coef_set"), sem("stored")

        out_t = out.rearrange("(t p) d -> p t d", p=P)
        bf_hi = lambda a: a.bitcast(BF16).rearrange("p (n two) -> p two n", two=2)[:, 1, :]

        with nc.Block() as block:
            @block.sync
            def _(sp):
                sp.dma_start(wa_f[:], wa).then_inc(cload, 16)
                sp.dma_start(b_bc[:], bout).then_inc(cload, 16)
                sp.dma_start(kvmask[:], mask).then_inc(cload, 16)
                sp.dma_start(rf_f[:], rfc).then_inc(rload, 16)
                sp.wait_ge(rload, 16)
                for s in range(3):
                    for h in range(4):
                        r0 = 32 * s + 8 * h
                        sp.dma_start(rf_f[r0:r0 + 8, F * h:F * h + F], rft).then_inc(rload, 16)

                def load(b, p):
                    need(sp, xload[p], 8 * (b - p))
                    sp.dma_start(xall[:, bass.ds(b * 2, 2), :], x[:, bass.ds(b * 2, 2), :]).then_inc(xload[p], 16)
                    need(sp, wsplit_lo, b - 1)
                    need(sp, wsplit_hi, b - 1)
                    sp.dma_start(w_st[:, p, :], wffn[:, bass.ds(b * WCH, WCH)]).then_inc(wload[p], 16)

                def store(b, p):
                    sp.wait_ge(q_read, reads_before(BANK_Q, Q_WOUT, b) + 1)
                    sp.dma_start(out_t[:, bass.ds(b * 2, 2), :], xall[:, bass.ds(b * 2, 2), :]).then_inc(stored, 16)

                pipeline(sp, [(0, load), (LAG, store)])

                sp.wait_ge(pset, 18)
                sp.dma_start(xs[E * CAP:E * CAP + SLOTS, :].rearrange("(h p) r -> p h r", p=P),
                             pad[:].bitcast(I32)).then_inc(tail, 16)
                sp.wait_ge(cnt_set, 1)
                for e in range(E):
                    n = nc.values_load(cnt_i[0:1, e:e + 1], engines=[mybir.EngineType.SP], min_val=0, max_val=T,
                                       skip_runtime_bounds_check_because="counts of tokens")
                    sp.dma_start(xs[bass.ds(n + e * CAP, SLOTS), :].rearrange("(h p) r -> p h r", p=P),
                                 pad[:].bitcast(I32)).then_inc(tail, 16)
                sp.wait_ge(tail, 16 * (E + 1))
                sp.wait_ge(tab_set, 1)
                for p in range(2):
                    sp.wait_ge(scat[p], 64 * NB // 2)

                def fetch(t, p):
                    need(sp, xl_turned, t - 1)
                    need(sp, odds1_set, t - 1)
                    r = nc.values_load(tab[0:1, 1, bass.ds(t, 1)], engines=[mybir.EngineType.SP], min_val=0,
                                       max_val=E * CAP, skip_runtime_bounds_check_because="clamped to the last tile")
                    sp.dma_start(xl[:, p].bitcast(I32), xs[bass.ds(r, SLOTS), :].rearrange("(h p) r -> p h r", p=P)).then_inc(
                        xl_load[p], 16)

                pipeline(sp, [(0, fetch)], 0, NX)

            def landed(b, p):
                return 8 * (b - p) + 16

            @block.gpsimd
            def _(pool):
                nc.gpsimd.memset(ident[:], 0.0).then_inc(pset, 1)
                nc.gpsimd.memset(tri[:], 0.0).then_inc(pset, 1)
                nc.gpsimd.memset(ones[:], 1.0).then_inc(pset, 1)
                nc.gpsimd.memset(mcum[:], 0.0).then_inc(pset, 1)
                nc.gpsimd.memset(ext[:, 0], 0.0).then_inc(pset, 1)
                nc.gpsimd.memset(ext[:, 1], 0.0).then_inc(pset, 1)
                nc.gpsimd.memset(vx[:, :, :, 0, :, 16:17], 1.0).then_inc(pset, 1)
                nc.gpsimd.memset(vx[:, :, :, 1, :, 16:17], 0.0).then_inc(pset, 1)
                nc.gpsimd.memset(rows[:], 0.0).then_inc(pset, 1)
                nc.gpsimd.iota(ids[:], [[P, NT]], base=0, channel_multiplier=1).then_inc(pset, 1)
                nc.gpsimd.iota(rank[:], [[-1, E]], base=E, channel_multiplier=0,
                               allow_small_or_imprecise_dtypes=True).then_inc(pset, 1)
                nc.gpsimd.iota(ebase[:], [[CAP, E]], base=0, channel_multiplier=0,
                               allow_small_or_imprecise_dtypes=True).then_inc(pset, 1)
                nc.gpsimd.iota(tnum[:], [[1, NX]], base=0, channel_multiplier=0,
                               allow_small_or_imprecise_dtypes=True).then_inc(pset, 1)
                nc.gpsimd.memset(pad[:], 0.0).then_inc(pset, 1)
                nc.gpsimd.memset(rs[:, :, 0:2], 1.0).then_inc(pset, 1)
                pool.wait_ge(pset, 15)
                nc.gpsimd.memset(pad[:, :, ID:ID + 2].bitcast(I32), PAD_ID).then_inc(pset, 1)
                nc.gpsimd.affine_select(out=ident[:], in_=ident[:], compare_op=ALU.not_equal, fill=1.0, base=0,
                                        pattern=[[-1, P]], channel_multiplier=1).then_inc(pset, 1)
                nc.gpsimd.affine_select(out=tri[:], in_=tri[:], compare_op=ALU.is_ge, fill=1.0, base=0,
                                        pattern=[[-1, P]], channel_multiplier=1).then_inc(pset, 1)

                def roots(it, q):
                    a, y, t, e = (rs[:, q, k] for k in range(4))
                    need(pool, xn_set, 2 * batches(it - 2, R_LN1))
                    need(pool, x2_set, 2 * batches(it - 2, R_LN2))
                    need(pool, nrm_set, batches(it - 2, R_NORM))
                    need(pool, ss_set, batches(it, R_NORM))
                    need(pool, ln2_st, 5 * batches(it, R_LN2))
                    wait_apart(pool, pool_passed, ln1_st, 5 * batches(it, R_LN1))
                    nc.gpsimd.tensor_scalar(y.bitcast(I32), a.bitcast(I32), -0.5, GUESS, ALU.mult,
                                            ALU.add).then_inc(rs_st, 1)
                    pool.wait_ge(rs_st, it * RS + 1)
                    nc.gpsimd.tensor_tensor(out=t, in0=a, in1=y, op=ALU.mult).then_inc(rs_st, 1)
                    pool.wait_ge(rs_st, it * RS + 2)
                    nc.gpsimd.tensor_tensor(out=e, in0=t, in1=y, op=ALU.mult).then_inc(rs_st, 1)
                    wait_apart(pool, pool_passed, rs_st, it * RS + 3)
                    nc.gpsimd.tensor_scalar(t, e, 0.375, -1.25, ALU.mult, ALU.add).then_inc(rs_st, 1)
                    pool.wait_ge(rs_st, it * RS + 4)
                    nc.gpsimd.tensor_tensor(out=t, in0=t, in1=e, op=ALU.mult).then_inc(rs_st, 1)
                    wait_apart(pool, pool_passed, rs_st, it * RS + 5)
                    nc.gpsimd.tensor_scalar(t, t, 1.875, None, ALU.add).then_inc(rs_st, 1)
                    pool.wait_ge(rs_st, it * RS + 6)
                    nc.gpsimd.tensor_tensor(out=y, in0=y, in1=t, op=ALU.mult).then_inc(rs_st, 1)
                    pool.wait_ge(rs_st, it * RS + 7)
                    nc.gpsimd.tensor_tensor(out=t, in0=a, in1=y, op=ALU.mult).then_inc(rs_st, 1)
                    pool.wait_ge(rs_st, it * RS + 8)
                    nc.gpsimd.tensor_tensor(out=e, in0=t, in1=y, op=ALU.mult).then_inc(rs_st, 1)
                    wait_apart(pool, pool_passed, rs_st, it * RS + 9)
                    nc.gpsimd.tensor_scalar(e, e, -0.5, 1.5, ALU.mult, ALU.add).then_inc(rs_st, 1)
                    pool.wait_ge(rs_st, it * RS + 10)
                    nc.gpsimd.tensor_tensor(out=y, in0=y, in1=e, op=ALU.mult).then_inc(rs_st, 1)

                def norms(b, p):
                    q = (p + R_NORM) % 2
                    need(pool, nrm_set, b - 1)
                    pool.wait_ge(rs_st, (b + R_NORM + 1) * RS)
                    nc.gpsimd.tensor_tensor(out=rs[:, q, 4, 0:64], in0=rs[:, q, 0, 0:64], in1=rs[:, q, 1, 0:64],
                                            op=ALU.mult).then_inc(nrm_st, 1)
                    need(pool, t_extk, b - 1)
                    wait_apart(pool, pool_passed, nrm_st, b * 2 + 1)
                    e = ext[:, p].rearrange("p t g c -> p (t g) c")
                    nv = rs[:, q, 4, 0:64].rearrange("p (tg h) -> p tg h", h=4)
                    nc.gpsimd.tensor_copy(e[:, :, 96:100], nv).then_inc(nrm_st, 1)
                    pool.wait_ge(nrm_st, b * 2 + 2)
                    nc.gpsimd.tensor_tensor(out=e[:, :, 100:104], in0=nv, in1=e[:, :, 96:100],
                                            op=ALU.subtract).then_inc(nrm_set, 1)

                def bias(b, p):
                    pool.wait_ge(xn_set, 2 * (b + 1))
                    for t in range(2):
                        v = xall[:, bass.ds(b * 2 + t, 1), :]
                        ins = nc.gpsimd.tensor_tensor(out=v, in0=v, in1=b_bc[:].rearrange("p (o d) -> p o d", o=1),
                                                      op=ALU.add)
                    ins.then_inc(bias_set, 1)

                def q_lo(b, p):
                    pool.wait_ge(z_exp, 4 * b + 1)
                    need(pool, o_done, b - 1)
                    nc.gpsimd.tensor_tensor(out=eq_lo[:, p, 0], in0=eq[:, p, 0], in1=bf_hi(eq[:, p, 0]),
                                            op=ALU.subtract).then_inc(eqlo_set[0], 1)

                def scatter(b, p):
                    pool.wait_ge(slot_set, b + 1)
                    pool.wait_ge(odds_set, 2 * (b + 1))
                    wait_apart(pool, pool_passed, rows_set, 2 * (b + 1))
                    for k in range(TOPK):
                        for t in range(2):
                            pool.indirect_dma_start(
                                out=xs[:, :], out_offset=bass.IndirectOffsetOnAxis(
                                    ap=slot[:, p, 2 * k + t:2 * k + t + 1], axis=0),
                                in_=rows[:, p, k, t, :].bitcast(I32), in_offset=None).then_inc(scat[p], 16)

                pool.wait_ge(cload, 48)
                pipeline(pool, [(None, roots), (2, norms), (5, scatter), (2, q_lo), (2, bias)])

                def put(t, p):
                    pool.wait_ge(y_set, 3 * (t + 1))
                    wait_apart(pool, pool_passed, y_scat[1 - p], 16 * (t + p))
                    for h in range(2):
                        pool.indirect_dma_start(
                            out=out[:, :], out_offset=bass.IndirectOffsetOnAxis(
                                ap=put_id[:, p, h:h + 1].bitcast(U32), axis=0),
                            in_=y[:, p, h, :], in_offset=None, bounds_check=T - 1,
                            oob_is_err=False, compute_op=ALU.add).then_inc(y_scat[p], 16)

                pool.wait_ge(tail, 16 * (E + 1))
                pool.wait_ge(stored, 16 * NB)
                pipeline(pool, [(2, put)], 2, NX)
                for p in range(2):
                    pool.wait_ge(y_scat[p], 32 * NX // 2)

            @block.scalar
            def _(act):
                act.wait_ge(cload, 48)
                nc.scalar.activation(wa_hi[:], wa_f[:], ACT.Copy, scale=W_SCALE).then_inc(wa_hi_set, 1)
                act.wait_ge(rload, 16 * 13)
                nc.scalar.activation(rf[:], rf_f[:], ACT.Copy).then_inc(rf_hi_set, 1)

                def xn_hi(b, p):
                    act.wait_ge(xn_set, 2 * (b + 1))
                    need(act, t_ln1, b - 1)
                    nc.scalar.activation(xn_s[:, p, 0], xn_f[:, p], ACT.Copy).then_inc(xnhi_set, 1)

                def xt_copy(b, p):
                    act.wait_ge(t_ln1, b + 1)
                    need(act, q_done, 2 * (b - 1))
                    nc.scalar.activation(xT[:, p].rearrange("p a n -> p (a n)"), bT[:, 0:512],
                                         ACT.Copy).then_inc(t_read, 1)

                def qkv_hi(t):
                    def stage(b, p):
                        act.wait_ge(q_done, 2 * b + t + 1)
                        if t == 0:
                            need(act, t_extk, b - 1)
                            need(act, kv_done, b - 1)
                            need(act, ss_set, b - 1)
                        qk = bQ[:, t, 0:256]
                        nc.scalar.activation(ext[:, p, t, :, 0:32], qk.rearrange("p (g c) -> p g c", g=8),
                                             ACT.Copy).then_inc(qhi_set, 1)
                        nc.scalar.activation(sq[:, p, t, :], qk, ACT.Square).then_inc(sq_set, 1)
                        nc.scalar.activation(vx[:, p, t, 0, :, 0:16],
                                             bQ[:, t, 256:384].rearrange("p (j c) -> p j c", j=8),
                                             ACT.Copy).then_inc(v_set, 1)
                    return stage

                def ext_copy(half, done):
                    def stage(b, p):
                        act.wait_ge(done, b + 1)
                        if half == 0:
                            need(act, z_done, 4 * (b - 1))
                        nc.scalar.activation(extT[:, p, 4 * half:4 * half + 4, :].rearrange("p g n -> p (g n)"),
                                             bT[:], ACT.Copy).then_inc(t_read, 1)
                    return stage

                def exp(k):
                    def stage(b, p):
                        act.wait_ge(z_done, 4 * b + k + 1)
                        if k < 2:
                            need(act, o_done, b - 1)
                            need(act, eqlo_set[k], b - 1)
                            dst = eq[:, p, k]
                        else:
                            need(act, kv_done, b)
                            dst = ek[:, k - 2]
                        nc.scalar.activation(dst, z[:, k % 2], ACT.Exp, bias=zbias[:, 0:1],
                                             scale=1.0 / (8 * W_SCALE)).then_inc(z_exp, 1)
                    return stage

                def att_hi(b, p):
                    act.wait_ge(m_read, reads_before(BANK_M, M_OUT, b) + 1)
                    need(act, t_att, b)
                    nc.scalar.activation(at_s[:, 0], at_f[:], ACT.Copy).then_inc(athi_set, 1)

                def att_copy(b, p):
                    act.wait_ge(t_att, b + 1)
                    need(act, w_done, b)
                    nc.scalar.activation(atT[:].rearrange("p a n -> p (a n)"), bT[:, 0:512],
                                         ACT.Copy).then_inc(t_read, 1)

                def x2_hi(b, p):
                    act.wait_ge(x2_set, 2 * (b + 1))
                    need(act, scat[p], 32 * (b - p))
                    need(act, rows_set, 2 * (b - 1))
                    nc.scalar.activation(rows[:, p, 0, :, 0:D], x2_f[:], ACT.Copy).then_inc(x2hi_set, 1)

                def x2_copy(b, p):
                    act.wait_ge(t_ln2, b + 1)
                    need(act, rt_done, b)
                    nc.scalar.activation(x2T[:].rearrange("p a n -> p (a n)"), bT[:, 0:512],
                                         ACT.Copy).then_inc(t_read, 1)

                def odds(b, p):
                    act.wait_ge(rt_st, b * 14 + 12)
                    need(act, scat[p], 32 * (b - p))
                    for k in range(TOPK):
                        nc.scalar.activation(rows[:, p, k, :, ODDS:ODDS + 2].bitcast(F32), gap[:, p].unsqueeze(2),
                                             ACT.Exp, scale=(1 - 2 * k) / W_SCALE).then_inc(odds_set, 1)

                def w_part(b, p):
                    act.wait_ge(wload[p], landed(b, p))
                    nc.scalar.activation(w_hi[:, bass.ds(b * WCH, WCH)], w_st[:, p, :], ACT.Copy,
                                         scale=W_SCALE).then_inc(wsplit_hi, 1)

                act.wait_ge(zb_set, 1)
                pipeline(act, [(0, w_part), (4, x2_hi), (2, ext_copy(0, t_extq)), (4, x2_copy), (3, att_hi),
                               (2, ext_copy(1, t_extk)), (3, att_copy), (2, exp(0)), (1, xt_copy), (2, exp(1)),
                               (2, exp(2)), (1, qkv_hi(0)), (1, qkv_hi(1)), (2, exp(3)), (4, odds), (0, xn_hi)])

                def silu(k):
                    def stage(t, p):
                        act.wait_ge(h_done, 2 * t + k + 1)
                        need(act, act_set, 2 * t + k - 1)
                        nc.scalar.activation(gate[:, k].rearrange("p (b n) -> p b n", b=2), z[:, k].rearrange(
                            "p (b w n) -> p b w n", b=2, w=2)[:, :, 0, :], ACT.Silu,
                            scale=1.0 / W_SCALE).then_inc(silu_set, 1)
                    return stage

                def act_high(k):
                    def stage(t, p):
                        act.wait_ge(act_set, 2 * t + k + 1)
                        need(act, y_done, t - 1)
                        nc.scalar.activation(act_hi[:, p, 2 * k:2 * k + 2].rearrange("p b n -> p (b n)"),
                                             act_f[:, k], ACT.Copy).then_inc(acthi_set, 1)
                    return stage

                act.wait_ge(tab_set, 1)
                pipeline(act, [(1, silu(0)), (1, silu(1)), (1, act_high(0)), (1, act_high(1))], 2, NX)

            @block.vector
            def _(dve):
                nc.vector.memset(zbias[:], Z_LN).then_inc(zb_set, 1)
                dve.wait_ge(wa_hi_set, 1)
                nc.vector.scalar_tensor_tensor(out=wa_lo[:], in0=wa_f[:], scalar=W_SCALE, in1=wa_hi[:],
                                               op0=ALU.mult, op1=ALU.subtract).then_inc(wa_lo_set, 1)
                dve.wait_ge(rf_hi_set, 1)
                nc.vector.tensor_tensor(out=rf[64:96, :], in0=rf_f[64:96, :], in1=rf[64:96, :],
                                        op=ALU.subtract).then_inc(rf_set, 1)
                dve.wait_ge(pset, 18)

                def stats(b, p, k, mv, lag, st, base):
                    for t in range(2):
                        nc.vector.bn_stats(bn[:, k, t, :], xall[:, bass.ds(b * 2 + t, 1), :].rearrange(
                            "p o d -> p (o d)")).then_inc(st, 1)
                    for t in range(2):
                        wait_apart(dve, dve_passed, st, base + t + 1)
                        nc.vector.bn_aggr(mv[:, p, t, :], bn[:, k, t, :]).then_inc(st, 1)
                    dve.wait_ge(st, base + 4)
                    need(dve, rs_st, (b + (lag - 1)) * RS)
                    nc.vector.tensor_scalar(rs[:, (p + lag) % 2, 0, 64 + 2 * k:66 + 2 * k], mv[:, p, :, 1], LN_EPS, None, ALU.add).then_inc(st, 1)

                def ln1_stats(b, p):
                    dve.wait_ge(xload[p], landed(b, p))
                    wait_apart(dve, dve_passed, xn_set, 2 * (b - 1))
                    stats(b, p, 0, mv1, R_LN1, ln1_st, 5 * b)

                def ln_1(b, p):
                    dve.wait_ge(rs_st, (b + R_LN1 + 1) * RS)
                    need(dve, xnhi_set, b - 1)
                    need(dve, xnlo_set, b - 1)
                    for t in range(2):
                        nc.vector.tensor_scalar(xn_f[:, p, t, :], xall[:, bass.ds(b * 2 + t, 1), :].rearrange(
                            "p o d -> p (o d)"), mv1[:, p, t, 0:1], rs[:, (p + R_LN1) % 2, 1, 64 + t:65 + t], ALU.subtract,
                            ALU.mult).then_inc(xn_set, 1)

                def ln1_lo(b, p):
                    dve.wait_ge(xnhi_set, b + 1)
                    dve.wait_ge(xn_set, 2 * (b + 1))
                    nc.vector.tensor_tensor(out=xn_s[:, p, 1], in0=xn_f[:, p], in1=xn_s[:, p, 0],
                                            op=ALU.subtract).then_inc(xnlo_set, 1)

                def split(t):
                    def stage(b, p):
                        dve.wait_ge(v_set, 2 * b + t + 1)
                        e = ext[:, p, t]
                        nc.vector.tensor_tensor(out=e[:, :, 32:64], in0=bQ[:, t, 0:256].rearrange(
                            "p (g c) -> p g c", g=8), in1=e[:, :, 0:32], op=ALU.subtract).then_inc(qlo_set, 1)
                        ins = nc.vector.tensor_tensor(
                            out=vx[:, p, t, 1, :, 0:16], in0=bQ[:, t, 256:384].rearrange("p (j c) -> p j c", j=8),
                            in1=vx[:, p, t, 0, :, 0:16], op=ALU.subtract)
                        if t == 1:
                            ins.then_inc(q_read, 1)
                    return stage

                def sums(b, p):
                    dve.wait_ge(v_set, 2 * (b + 1))
                    e = ext[:, p].rearrange("p t g c -> p (t g) c")
                    nc.vector.tensor_copy(e[:, :, 64:96], e[:, :, 0:32]).then_inc(slab2_set, 1)
                    need(dve, rs_st, (b + (R_NORM - 1)) * RS)
                    need(dve, nrm_st, b * 2 - 3)
                    nc.vector.tensor_reduce(rs[:, (p + R_NORM) % 2, 0, 0:64], sq[:, p].rearrange("p t (h d) -> p (t h) d", d=HD),
                                            AX.X, ALU.add).then_inc(ss_set, 1)

                def exp_lo(k):
                    def stage(b, p):
                        dve.wait_ge(z_exp, 4 * b + k + 1)
                        if k < 2:
                            src, dst, done = eq[:, p, k], eq_lo[:, p, k], eqlo_set[1]
                            need(dve, o_done, b - 1)
                        else:
                            src, dst, done = ek[:, k - 2], ek_lo[:, k - 2], eklo_set
                            need(dve, kv_done, b)
                        nc.vector.tensor_tensor(out=dst, in0=src, in1=bf_hi(src), op=ALU.subtract).then_inc(done, 1)
                    return stage

                def kv_parts(b, p):
                    dve.wait_ge(kv_done, b + 1)
                    need(dve, o_done, b)
                    need(dve, kv_st, 3 * b)
                    nc.vector.tensor_tensor(out=kvm[:, :, 0:16], in0=m_kv[:, :, 0:16],
                                            in1=kvmask[:, 0:16].unsqueeze(1).to_broadcast([P, 8, 16]), op=ALU.mult)
                    nc.vector.tensor_tensor(out=kvm[:, :, 16:18], in0=m_kv[:, :, 16:17].to_broadcast([P, 8, 2]),
                                            in1=kvmask[:, 16:18].unsqueeze(1).to_broadcast([P, 8, 2]),
                                            op=ALU.mult).then_inc(m_read, 1)
                    dve.wait_ge(m_read, reads_before(BANK_M, M_KV, b) + 1)
                    nc.vector.tensor_copy(kvp[:, 0], kvm[:]).then_inc(kv_st, 1)
                    dve.wait_ge(kv_st, 3 * b + 1)
                    nc.vector.tensor_tensor(out=kvr[:], in0=kvm[:], in1=kvp[:, 0], op=ALU.subtract).then_inc(kv_st, 1)
                    dve.wait_ge(kv_st, 3 * b + 2)
                    nc.vector.tensor_copy(kvp[:, 1], kvr[:]).then_inc(kv_st, 1)
                    dve.wait_ge(kv_st, 3 * b + 3)
                    nc.vector.tensor_tensor(out=kvp[:, 2], in0=kvr[:], in1=kvp[:, 1], op=ALU.subtract).then_inc(kv_set, 1)

                def divide(b, p):
                    need(dve, athi_set, b)
                    need(dve, atlo_set, b)
                    need(dve, at_st, 2 * b)
                    dve.wait_ge(o_done, b + 1)
                    o = m_out.rearrange("p t j c -> p (t j) c")
                    nc.vector.tensor_scalar(den[:], o[:, :, 16:18], 1e-6 * Z2, None, ALU.add).then_inc(at_st, 1)
                    dve.wait_ge(at_st, 2 * b + 1)
                    nc.vector.reciprocal(rden[:], den[:]).then_inc(at_st, 1)
                    dve.wait_ge(at_st, 2 * b + 2)
                    nc.vector.tensor_tensor(
                        out=at_f[:].rearrange("p t (j h c) -> p (t j) h c", j=8, h=2),
                        in0=o[:, :, 0:16].rearrange("p j (h c) -> p j h c", h=2),
                        in1=rden[:].unsqueeze(3).to_broadcast([P, 16, 2, 8]), op=ALU.mult).then_inc(m_read, 1)

                def att_lo(b, p):
                    dve.wait_ge(athi_set, b + 1)
                    dve.wait_ge(m_read, reads_before(BANK_M, M_OUT, b) + 1)
                    nc.vector.tensor_tensor(out=at_s[:, 1], in0=at_f[:], in1=at_s[:, 0],
                                            op=ALU.subtract).then_inc(atlo_set, 1)

                def residual(b, p):
                    dve.wait_ge(bias_set, b + 1)
                    dve.wait_ge(w_done, b + 1)
                    v = xall[:, bass.ds(b * 2, 2), :]
                    nc.vector.scalar_tensor_tensor(out=v, in0=bQ[:, :, 384:512], scalar=1.0 / (W_SCALE * W_SCALE),
                                                   in1=v, op0=ALU.mult, op1=ALU.add).then_inc(q_read, 1)

                def ln2_stats(b, p):
                    dve.wait_ge(q_read, reads_before(BANK_Q, Q_WOUT, b) + 1)
                    wait_apart(dve, dve_passed, x2_set, 2 * (b - 1))
                    stats(b, p, 1, mv2, R_LN2, ln2_st, 5 * b)

                def ln_2(b, p):
                    dve.wait_ge(rs_st, (b + R_LN2 + 1) * RS)
                    need(dve, x2hi_set, b)
                    need(dve, x2lo_set, b)
                    for t in range(2):
                        nc.vector.tensor_scalar(x2_f[:, t, :], xall[:, bass.ds(b * 2 + t, 1), :].rearrange(
                            "p o d -> p (o d)"), mv2[:, p, t, 0:1], rs[:, (p + R_LN2) % 2, 1, 66 + t:67 + t], ALU.subtract,
                            ALU.mult).then_inc(x2_set, 1)

                def ln2_lo(b, p):
                    dve.wait_ge(x2hi_set, b + 1)
                    dve.wait_ge(x2_set, 2 * (b + 1))
                    nc.vector.tensor_tensor(out=rows[:, p, 0, :, D:2 * D], in0=x2_f[:], in1=rows[:, p, 0, :, 0:D],
                                            op=ALU.subtract).then_inc(x2lo_set, 1)

                def fill_rows(b, p):
                    dve.wait_ge(x2lo_set, b + 1)
                    nc.vector.tensor_copy(rows[:, p, 1, :, 0:2 * D], rows[:, p, 0, :, 0:2 * D]).then_inc(rows_set, 1)
                    nc.vector.tensor_copy(rows[:, p, :, :, ID:ID + 2].bitcast(I32), ids[:, bass.ds(b * 2, 2)].unsqueeze(
                        1).unsqueeze(3).to_broadcast([P, TOPK, 2, 1])).then_inc(rows_set, 1)

                def route_a(b, p):
                    n = 14 * b
                    bc = lambda a: a.unsqueeze(2).to_broadcast([P, 2, E])
                    rk = rank[:].unsqueeze(1).to_broadcast([P, 2, E])
                    dve.wait_ge(rt_done, b + 1)
                    need(dve, rt_st, n)
                    nc.vector.tensor_copy(lg[:], m_rt).then_inc(m_read, 1)
                    dve.wait_ge(m_read, reads_before(BANK_M, M_RT, b) + 1)
                    src = lg
                    for k in range(2):
                        nc.vector.tensor_reduce(top[:, k], src[:], AX.X, ALU.max).then_inc(rt_st, 1)
                        dve.wait_ge(rt_st, n + 6 * k + 1)
                        nc.vector.tensor_tensor(out=cand[:, k, 0], in0=src[:], in1=bc(top[:, k]),
                                                op=ALU.is_equal).then_inc(rt_st, 1)
                        dve.wait_ge(rt_st, n + 6 * k + 2)
                        nc.vector.tensor_tensor(out=cand[:, k, 1], in0=cand[:, k, 0], in1=rk, op=ALU.mult).then_inc(rt_st, 1)
                        dve.wait_ge(rt_st, n + 6 * k + 3)
                        nc.vector.tensor_reduce(top[:, 2 + k], cand[:, k, 1], AX.X, ALU.max).then_inc(rt_st, 1)
                        dve.wait_ge(rt_st, n + 6 * k + 4)
                        nc.vector.tensor_tensor(out=pick[:, k], in0=cand[:, k, 1], in1=bc(top[:, 2 + k]),
                                                op=ALU.is_equal).then_inc(rt_st, 1)
                        dve.wait_ge(rt_st, n + 6 * k + 5)
                        if k == 0:
                            nc.vector.scalar_tensor_tensor(out=lg2[:], in0=pick[:, 0], scalar=-3.0e38, in1=lg[:],
                                                           op0=ALU.mult, op1=ALU.add).then_inc(rt_st, 1)
                            dve.wait_ge(rt_st, n + 6)
                            src = lg2
                    need(dve, odds_set, 2 * (b - 1))
                    nc.vector.tensor_tensor(out=gap[:, p], in0=top[:, 1], in1=top[:, 0],
                                            op=ALU.subtract).then_inc(rt_st, 1)
                    need(dve, pos_done, b - 1)
                    nc.vector.tensor_tensor(out=both[:, p], in0=pick[:, 0], in1=pick[:, 1],
                                            op=ALU.add).then_inc(both_set, 1)

                def route_b(b, p):
                    dve.wait_ge(pos_done, b + 1)
                    nc.vector.tensor_tensor(out=where[:], in0=m_pos, in1=ebase[:].unsqueeze(1).to_broadcast([P, 2, E]),
                                            op=ALU.add).then_inc(m_read, 1)
                    nc.vector.tensor_tensor(out=cum1[:], in0=mcum[:], in1=both[:, p, 0], op=ALU.add).then_inc(cum_st, 1)
                    dve.wait_ge(m_read, reads_before(BANK_M, M_POS, b) + 1)
                    for k in range(TOPK):
                        ins = nc.vector.tensor_tensor(out=hit[:, k], in0=pick[:, k], in1=where[:], op=ALU.mult)
                    ins.then_inc(rt_st, 1)
                    dve.wait_ge(cum_st, b + 1)
                    nc.vector.tensor_tensor(out=mcum[:], in0=cum1[:], in1=both[:, p, 1], op=ALU.add).then_inc(cum_set, 1)
                    dve.wait_ge(rt_st, 14 * b + 13)
                    nc.vector.tensor_reduce(slot_f[:], hit[:].rearrange("p k t e -> p (k t) e"), AX.X,
                                            ALU.add).then_inc(rt_st, 1)
                    dve.wait_ge(rt_st, 14 * b + 14)
                    need(dve, scat[p], 32 * (b - p))
                    nc.vector.tensor_copy(slot[:, p], slot_f[:]).then_inc(slot_set, 1)

                def w_part(b, p):
                    dve.wait_ge(wsplit_hi, b + 1)
                    w = bass.ds(b * WCH, WCH)
                    nc.vector.scalar_tensor_tensor(out=w_lo[:, w], in0=w_st[:, p, :], scalar=W_SCALE, in1=w_hi[:, w],
                                                   op0=ALU.mult, op1=ALU.subtract).then_inc(wsplit_lo, 1)

                pipeline(dve, [(4, ln_2), (4, ln2_lo), (3, divide), (0, ln1_stats), (4, fill_rows), (3, att_lo),
                               (4, route_a), (3, residual), (0, w_part), (3, ln2_stats), (2, exp_lo(2)), (1, sums),
                               (1, split(0)), (2, exp_lo(3)), (2, exp_lo(1)), (2, kv_parts), (4, route_b), (0, ln_1),
                               (1, split(1)), (0, ln1_lo)])

                n = [0]

                def chain(ins):
                    n[0] += 1
                    ins.then_inc(ph2, 1)
                    dve.wait_ge(ph2, n[0])

                dve.wait_ge(cnt_done, 1)
                chain(nc.vector.tensor_copy(cnt[:], bM[:, 0:E]))
                nc.vector.tensor_copy(cnt_i[:], cnt[:]).then_inc(cnt_set, 1)
                chain(nc.vector.tensor_scalar(up_i[:, 0], cnt[:], float(SLOTS - 1), None, ALU.add))
                chain(nc.vector.tensor_scalar(up_i[:, 1], up_i[:, 0], SLOTS.bit_length() - 1, None,
                                              ALU.logical_shift_right))
                chain(nc.vector.tensor_copy(ntile[:], up_i[:, 1]))
                chain(nc.vector.tensor_copy(ends[:, 0:1], ntile[:, 0:1]))
                for e in range(1, E):
                    chain(nc.vector.tensor_tensor(out=ends[:, e:e + 1], in0=ends[:, e - 1:e], in1=ntile[:, e:e + 1],
                                                  op=ALU.add))
                chain(nc.vector.tensor_scalar(skip[:], ntile[:], -float(SLOTS), float(CAP), ALU.mult, ALU.add))
                chain(nc.vector.tensor_tensor(out=past[:], in0=tnum[:].unsqueeze(2).to_broadcast([P, NX, E]),
                                              in1=ends[:].unsqueeze(1).to_broadcast([P, NX, E]), op=ALU.is_ge))
                chain(nc.vector.tensor_tensor(out=jump[:], in0=past[:], in1=skip[:].unsqueeze(1).to_broadcast(
                    [P, NX, E]), op=ALU.mult))
                chain(nc.vector.tensor_reduce(tab_f[:, 0, 0], past[:], AX.X, ALU.add))
                chain(nc.vector.tensor_reduce(tab_f[:, 0, 1], jump[:], AX.X, ALU.add))
                chain(nc.vector.scalar_tensor_tensor(out=tab_f[:, 1, 1], in0=tnum[:], scalar=float(SLOTS),
                                                     in1=tab_f[:, 0, 1], op0=ALU.mult, op1=ALU.add))
                chain(nc.vector.tensor_scalar(tab[:, 0], tab_f[:, 0, 0], float(E - 1), None, ALU.min))
                nc.vector.tensor_scalar(tab[:, 1], tab_f[:, 1, 1], float(E * CAP), None, ALU.min).then_inc(tab_set, 1)

                def xl_copy(t, p):
                    dve.wait_ge(xl_turned, t + 1)
                    need(dve, h_done, 2 * (t - 1))
                    nc.vector.tensor_copy(xlT[:, p].rearrange("p a n -> p (a n)"), bT[:, 0:512]).then_inc(xlT_set, 1)
                    dve.wait_ge(xl_load[p], 8 * (t - p) + 16)
                    nc.vector.tensor_copy(row_id[:, bass.ds(t, 1), :].unsqueeze(3),
                                          xl[:, p, :, ID:ID + 2].bitcast(I32).unsqueeze(1)).then_inc(id_kept, 1)
                    nc.vector.tensor_scalar(odds1[:, bass.ds(t, 1), :].unsqueeze(3),
                                            xl[:, p, :, ODDS:ODDS + 2].bitcast(F32).unsqueeze(1), 1.0,
                                            W_SCALE * W_SCALE, ALU.add, ALU.mult).then_inc(odds1_set, 1)
                    dve.wait_ge(odds1_set, t + 1)
                    nc.vector.reciprocal(coef[:, bass.ds(t, 1), :], odds1[:, bass.ds(t, 1), :]).then_inc(coef_set, 1)

                def gated(k):
                    def stage(t, p):
                        dve.wait_ge(silu_set, 2 * t + k + 1)
                        need(dve, acthi_set, 2 * t + k - 1)
                        need(dve, actlo_set, 2 * t + k - 1)
                        nc.vector.tensor_tensor(out=act_f[:, k].rearrange("p (b n) -> p b n", b=2),
                                                in0=z[:, k].rearrange("p (b w n) -> p b w n", b=2, w=2)[:, :, 1, :],
                                                in1=gate[:, k].rearrange("p (b n) -> p b n", b=2),
                                                op=ALU.mult).then_inc(act_set, 1)
                    return stage

                def act_low(k):
                    def stage(t, p):
                        dve.wait_ge(acthi_set, 2 * t + k + 1)
                        nc.vector.tensor_tensor(
                            out=act_lo[:, p, 2 * k:2 * k + 2].rearrange("p b n -> p (b n)"), in0=act_f[:, k],
                            in1=act_hi[:, p, 2 * k:2 * k + 2].rearrange("p b n -> p (b n)"),
                            op=ALU.subtract).then_inc(actlo_set, 1)
                    return stage

                def y_copy(t, p):
                    dve.wait_ge(y_done, t + 1)
                    need(dve, y_scat[p], 16 * (t - p))
                    dve.wait_ge(coef_set, t + 1)
                    for h in range(2):
                        nc.vector.tensor_scalar(y[:, p, h, :], bQ[:, p, P * h:P * h + P], coef[:, bass.ds(t, 1), h],
                                                None, ALU.mult).then_inc(y_set, 1)
                    dve.wait_ge(id_kept, t + 1)
                    nc.vector.tensor_copy(put_id[:, p, :].unsqueeze(1), row_id[:, bass.ds(t, 1), :]).then_inc(y_set, 1)

                pipeline(dve, [(1, gated(0)), (0, xl_copy), (1, gated(1)), (1, act_low(0)), (1, act_low(1)),
                               (2, y_copy)], 2, NX)

            @block.tensor
            def _(pe):
                mm = nc.tensor.matmul
                pe.wait_ge(pset, 18)
                pe.wait_ge(wa_lo_set, 1)
                pe.wait_ge(rf_set, 1)

                def free_bank(s, bank, k, b):
                    need(pe, s, reads_before(bank, k, b))

                def three(out_, hi, lo, w_h, w_l, start):
                    mm(out_, hi, w_h, start=start, stop=False, skip_group_check=True)
                    mm(out_, hi, w_l, start=False, stop=False, skip_group_check=True)
                    return mm(out_, lo, w_h, start=False, stop=True, skip_group_check=True)

                def turn(src, n):
                    for k in range(n):
                        last = nc.tensor.transpose(bT[:, P * k:P * k + P], src(k), ident[:])
                    return last

                def ext_turn(half, k, done):
                    def stage(b, p):
                        pe.wait_ge(nrm_set, b + 1)
                        pe.wait_ge(slab2_set, b + 1)
                        pe.wait_ge(qlo_set, 2 * (b + 1))
                        free_bank(t_read, BANK_T, k, b)
                        turn(lambda n: ext[:, p, n % 2, 4 * half + n // 2, :], 8).then_inc(done, 1)
                    return stage

                def ln1_turn(b, p):
                    pe.wait_ge(xnlo_set, b + 1)
                    free_bank(t_read, BANK_T, T_LN1, b)
                    turn(lambda n: xn_s[:, p, n // 2, n % 2, :], 4).then_inc(t_ln1, 1)

                def att_turn(b, p):
                    pe.wait_ge(atlo_set, b + 1)
                    free_bank(t_read, BANK_T, T_ATT, b)
                    turn(lambda n: at_s[:, n // 2, n % 2, :], 4).then_inc(t_att, 1)

                def ln2_turn(b, p):
                    pe.wait_ge(x2lo_set, b + 1)
                    free_bank(t_read, BANK_T, T_LN2, b)
                    turn(lambda n: rows[:, p, 0, n % 2, D * (n // 2):D * (n // 2) + D], 4).then_inc(t_ln2, 1)

                def qkv(b, p):
                    pe.wait_ge(t_read, reads_before(BANK_T, T_LN1, b) + 1)
                    free_bank(q_read, BANK_Q, Q_QKV, b)
                    for t in range(2):
                        c = slice(P * t, P * t + P)
                        three(bQ[:, t, 0:384], xT[:, p, 0, c], xT[:, p, 1, c], wa_hi[:, 0:384], wa_lo[:, 0:384],
                              True).then_inc(q_done, 1)

                def features(k):
                    def stage(b, p):
                        pe.wait_ge(t_read, reads_before(BANK_T, T_EXTQ if k < 2 else T_EXTK, b) + 1)
                        need(pe, z_exp, 4 * b + k - 1)
                        for n in range(4):
                            o = z[:, k % 2, 256 * n:256 * n + 256]
                            if k < 2:
                                last = mm(o, rf[:, P * (n % 2):P * (n % 2) + P], extT[:, p, 2 * k + n // 2, :],
                                          start=True, stop=True, skip_group_check=True)
                            else:
                                last = mm(o, extT[:, p, 4 + n, P * (k - 2):P * (k - 1)], rf[:], start=True, stop=True,
                                          skip_group_check=True)
                        last.then_inc(z_done, 1)
                    return stage

                def kv(b, p):
                    free_bank(m_read, BANK_M, M_KV, b)
                    pe.wait_ge(q_read, reads_before(BANK_Q, Q_QKV, b) + 1)
                    for t in range(2):
                        pe.wait_ge(eklo_set, 2 * b + t + 1)
                        for j in range(8):
                            f = slice(P * j, P * j + P)
                            for e, c in ((bf_hi(ek[:, t, f]), 0), (bf_hi(ek[:, t, f]), 1), (ek_lo[:, t, f], 0),
                                         (ek_lo[:, t, f], 1)):
                                first = t == 0 and j == 0 and c == 0 and e.dtype == BF16
                                last = mm(m_kv[:, j, :], e, vx[:, p, t, c, j, :], start=first, stop=False,
                                          skip_group_check=True)
                    last.then_inc(kv_done, 1)

                def attend(b, p):
                    free_bank(m_read, BANK_M, M_OUT, b)
                    pe.wait_ge(kv_set, b + 1)
                    pe.wait_ge(eqlo_set[0], b + 1)
                    pe.wait_ge(eqlo_set[1], b + 1)
                    for t in range(2):
                        for j in range(8):
                            f = slice(256 * (j % 4) + P * t, 256 * (j % 4) + P * t + P)
                            n = 0
                            for e in (bf_hi(eq[:, p, j // 4, f]), eq_lo[:, p, j // 4, f]):
                                for c in range(3):
                                    last = mm(m_out[:, t, j, :], e, kvp[:, c, j, :], start=(t + j + n == 0),
                                              stop=False, skip_group_check=True)
                                    n += 1
                    last.then_inc(o_done, 1)

                def w_out(b, p):
                    pe.wait_ge(t_read, reads_before(BANK_T, T_ATT, b) + 1)
                    free_bank(q_read, BANK_Q, Q_WOUT, b)
                    for t in range(2):
                        c = slice(P * t, P * t + P)
                        last = three(bQ[:, t, 384:512], atT[:, 0, c], atT[:, 1, c], wa_hi[:, 384:512],
                                     wa_lo[:, 384:512], True)
                    last.then_inc(w_done, 1)

                def router(b, p):
                    pe.wait_ge(t_read, reads_before(BANK_T, T_LN2, b) + 1)
                    free_bank(m_read, BANK_M, M_RT, b)
                    for t in range(2):
                        c = slice(P * t, P * t + P)
                        last = three(m_rt[:, t, :], x2T[:, 0, c], x2T[:, 1, c], wa_hi[:, 512:520], wa_lo[:, 512:520],
                                     t == 0)
                    last.then_inc(rt_done, 1)

                def positions(b, p):
                    pe.wait_ge(both_set, b + 1)
                    need(pe, cum_set, b)
                    free_bank(m_read, BANK_M, M_POS, b)
                    mm(m_pos[:, 0, :], tri[:], both[:, p, 0, :], start=True, stop=False, skip_group_check=True)
                    mm(m_pos[:, 0, :], ones[:], mcum[:], start=False, stop=True, skip_group_check=True)
                    mm(m_pos[:, 1, :], tri[:], both[:, p, 1, :], start=False, stop=False, skip_group_check=True)
                    mm(m_pos[:, 1, :], ones[:], mcum[:], start=False, stop=False, skip_group_check=True)
                    mm(m_pos[:, 1, :], ones[:], both[:, p, 0, :], start=False, stop=True,
                       skip_group_check=True).then_inc(pos_done, 1)

                pipeline(pe, [(3, attend), (2, ext_turn(0, T_EXTQ, t_extq)), (4, ln2_turn),
                              (2, ext_turn(1, T_EXTK, t_extk)), (4, router), (2, features(0)), (3, att_turn),
                              (2, features(1)), (1, ln1_turn), (3, w_out), (2, features(2)), (1, qkv),
                              (2, features(3)), (2, kv), (4, positions)])

                pe.wait_ge(cum_set, NB)
                need(pe, m_read, reads_before(BANK_M, M_OUT, NB + LAG))
                mm(bM[:, 0:E], ones[:], mcum[:], start=True, stop=True, skip_group_check=True).then_inc(cnt_done, 1)

                w_h = w_hi[:].rearrange("p (e w n) -> p e w n", e=E, w=3)
                w_l = w_lo[:].rearrange("p (e w n) -> p e w n", e=E, w=3)
                expert = {}

                def rows_turn(t, p):
                    pe.wait_ge(xl_load[p], 8 * (t - p) + 16)
                    need(pe, xlT_set, t)
                    turn(lambda n: xl[:, p, n % 2, D * (n // 2):D * (n // 2) + D], 4).then_inc(xl_turned, 1)

                def load_expert(t):
                    return nc.values_load(tab[0:1, 0, bass.ds(t, 1)], engines=[mybir.EngineType.PE], min_val=0,
                                          max_val=E - 1, skip_runtime_bounds_check_because="clamped to the last expert")

                def hidden(k):
                    def stage(t, p):
                        if k == 0:
                            expert[1] = load_expert(t)
                            pe.wait_ge(xlT_set, t + 1)
                        e = expert[1]
                        need(pe, act_set, 2 * t + k - 1)
                        for b in range(2):
                            for w in range(2):
                                c = slice(256 * k + P * b, 256 * k + P * b + P)
                                o = z[:, k, 512 * b + 256 * w:512 * b + 256 * w + 256]
                                mm(o, w_h[:, bass.ds(e, 1), w, c].rearrange("p o n -> p (o n)"), xlT[:, p, 0, :],
                                   start=(w == 0), stop=False, skip_group_check=True)
                                mm(o, w_h[:, bass.ds(e, 1), w, c].rearrange("p o n -> p (o n)"), xlT[:, p, 1, :],
                                   start=False, stop=False, skip_group_check=True)
                                last = mm(o, w_l[:, bass.ds(e, 1), w, c].rearrange("p o n -> p (o n)"),
                                          xlT[:, p, 0, :], start=False, stop=True, skip_group_check=True)
                        last.then_inc(h_done, 1)
                    return stage

                def output(t, p):
                    e = load_expert(t)
                    pe.wait_ge(actlo_set, 2 * (t + 1))
                    need(pe, y_set, 3 * (t - 1))
                    for h in range(2):
                        o = bQ[:, p, P * h:P * h + P]
                        c = slice(P * h, P * h + P)
                        for b in range(4):
                            w = slice(P * b, P * b + P)
                            w2h = w_h[:, bass.ds(e, 1), 2, w].rearrange("p o n -> p (o n)")
                            w2l = w_l[:, bass.ds(e, 1), 2, w].rearrange("p o n -> p (o n)")
                            mm(o, act_hi[:, p, b, c], w2h, start=(h + b == 0), stop=False, skip_group_check=True)
                            mm(o, act_hi[:, p, b, c], w2l, start=False, stop=False, skip_group_check=True)
                            last = mm(o, act_lo[:, p, b, c], w2h, start=False, stop=True, skip_group_check=True)
                    last.then_inc(y_done, 1)

                pe.wait_ge(tab_set, 1)
                pe.wait_ge(wsplit_lo, NB)
                need(pe, z_exp, 4 * NB)
                need(pe, t_read, reads_before(BANK_T, T_EXTQ, NB + LAG))
                need(pe, q_read, 2 * NB)
                pipeline(pe, [(0, rows_turn), (1, hidden(0)), (1, hidden(1)), (2, output)], 2, NX)


def kernel(L0_attn_x, L0_attn_w_qkv, L0_attn_w_out, L0_attn_b_out, L0_attn_random_features, L0_ffn_gate_w, L0_ffn_w1,
           L0_ffn_w3, L0_ffn_w2):
    import numpy as np
    import concourse.bacc as bacc
    from concourse.bass_utils import run_bass_kernel_spmd

    cont = np.ascontiguousarray
    wa = np.concatenate([np.asarray(w).T for w in (L0_attn_w_qkv, L0_attn_w_out, L0_ffn_gate_w)], axis=1)
    w13 = [np.asarray(w).transpose(2, 0, 1) for w in (L0_ffn_w1, L0_ffn_w3)]
    w2 = np.asarray(L0_ffn_w2).transpose(2, 0, 1).reshape(4, P, E, D).transpose(1, 2, 0, 3).reshape(P, E, 4 * D)
    rfc = np.zeros((P, 4 * F), np.float32)
    for h in range(4):
        for part in range(2):
            rfc[96 + 4 * part + h, F * h:F * h + F] = -8.0
    mask = np.zeros((P, 18), np.float32)
    for r in range(P):
        mask[r, HD * (r // F):HD * (r // F) + HD] = 1.0
        mask[r, 16 + r // F] = 1.0
    arrays = {
        "x": cont(np.asarray(L0_attn_x).reshape(T, D)),
        "wa": cont(wa),
        "bout": cont(np.broadcast_to(np.asarray(L0_attn_b_out), (P, D))),
        "rft": cont(np.asarray(L0_attn_random_features).T),
        "rfc": rfc,
        "wffn": cont(np.concatenate([*w13, w2], axis=2).reshape(P, E * 3 * HID)),
        "mask": mask,
    }
    nc = bacc.Bacc("TRN2", target_bir_lowering=False, num_devices=1)
    ins = {n: nc.dram_tensor(n, a.shape, F32, kind="ExternalInput").ap() for n, a in arrays.items()}
    out = nc.dram_tensor("out", (T, D), F32, kind="ExternalOutput").ap()
    xs = nc.dram_tensor("xs", (E * CAP + SLOTS, ROW // 2), mybir.dt.int32, kind="Internal").ap()
    ins["x"] = ins["x"].rearrange("(t p) d -> p t d", p=P)
    build(nc, **ins, out=out, xs=xs)
    r = run_bass_kernel_spmd(nc, [arrays], core_ids=[0])
    return r.results[0]["out"].reshape(L0_attn_x.shape)
```

```python
from contextlib import ExitStack

import concourse.bass as bass
from concourse import mybir

F32, F16, BF16 = mybir.dt.float32, mybir.dt.float16, mybir.dt.bfloat16
I32, U32 = mybir.dt.int32, mybir.dt.uint32
ACT, ALU, AX = mybir.ActivationFunctionType, mybir.AluOpType, mybir.AxisListType

P = 128
T = 8192
D = 128
H, HD, F = 16, 8, 64
NT = T // P
NB = 32
E, HID, TOPK = 8, 512, 2
SLOTS = 256
NX = T * TOPK // SLOTS + E
CAP = T + SLOTS
ROW = 264
ID, ODDS = 256, 258
PAD_ID = T
W_SCALE = 16.0
Z_LN = 8 * 0.6931471805599453
Z2 = 65536.0
LN_EPS = 1e-5
WCH = E * 3 * HID // NB
LAG = 5
RS = 11
GUESS = float(0x5F3759DF)
R_LN1, R_NORM, R_LN2 = 1, 2, 4


def need(eng, sem, value):
    if isinstance(value, int) and value <= 0:
        return
    eng.wait_ge(sem, value)


def wait_apart(eng, passed, sem, value):
    if isinstance(value, int):
        return need(eng, sem, value)
    eng.wait_ge(sem, value).then_inc(passed, 1)


def pipeline(eng, stages, last=LAG, n=NB):
    last += last % 2

    def iterate(it):
        for lag, stage in stages:
            if lag is None:
                stage(it, it % 2)
            elif 0 <= it - lag < n:
                stage(it - lag, (it - lag) % 2)

    for it in range(last + 2):
        iterate(it)
    with eng.Fori(last // 2 + 1, n // 2) as i:
        for u in range(2):
            for lag, stage in stages:
                lag = lag or 0
                stage(i * 2 + (u - lag), (u - lag) % 2)
    for it in range(n, n + last):
        iterate(it)


def batches(it, lag):
    return max(0, min(it - lag + 1, NB)) if isinstance(it, int) else it - lag + 1


def reads_before(uses, k, b):
    it = b + uses[k][0]
    if isinstance(b, int):
        return sum(n * min(max(it - lag + (j < k), 0), NB) for j, (lag, n) in enumerate(uses))
    return it * sum(n for _, n in uses) + sum(n * ((j < k) - lag) for j, (lag, n) in enumerate(uses))


BANK_T = [(2, 1), (4, 1), (3, 1), (2, 1), (1, 1)]
T_EXTQ, T_LN2, T_ATT, T_EXTK, T_LN1 = range(5)
BANK_Q = [(3, 1), (1, 1)]
Q_WOUT, Q_QKV = range(2)
BANK_M = [(3, 1), (4, 1), (2, 1), (4, 1)]
M_OUT, M_RT, M_KV, M_POS = range(4)


def build(nc, x, wa, bout, features_w, wffn, mask, out, xs):
    with ExitStack() as ctx:
        def sb(name, shape, dt):
            return ctx.enter_context(nc.sbuf_tensor(name, shape, dt))

        def psum(name, shape, dt):
            return ctx.enter_context(nc.psum_tensor(name, shape, dt))

        def sem(name):
            return ctx.enter_context(nc.semaphore(name))

        ident = sb("ident", [P, P], F16)
        tri = sb("tri", [P, P], F16)
        ones = sb("ones", [P, P], F16)
        wa_f = sb("wa_f", [P, 520], F32)
        wa_hi = sb("wa_hi", [P, 520], F16)
        wa_lo = sb("wa_lo", [P, 520], F16)
        rf_f = sb("rf_f", [P, 4 * F], F32)
        rf = sb("rf", [P, 4 * F], F16)
        b_bc = sb("b_bc", [P, D], F32)
        kvmask = sb("kvmask", [P, 18], F32)
        rank = sb("rank", [P, E], F32)
        ebase = sb("ebase", [P, E], F32)
        ids = sb("ids", [P, NT], I32)
        w_st = sb("w_st", [P, 2, WCH], F32)
        w_hi = sb("w_hi", [P, E * 3 * HID], F16)
        w_lo = sb("w_lo", [P, E * 3 * HID], F16)

        xall = sb("xall", [P, NT, D], F32)
        mcum = sb("mcum", [P, E], F16)

        bn = sb("bn", [P, 2, 2, 6], F32)
        mv1 = sb("mv1", [P, 2, 2, 2], F32)
        rs = sb("rs", [P, 2, 5, 68], F32)
        xn_f = sb("xn_f", [P, 2, 2, D], F32)
        xn_s = sb("xn_s", [P, 2, 2, 2, D], F16)
        xT = sb("xT", [P, 2, 2, 256], F16)
        ext = sb("ext", [P, 2, 2, 8, P], F16)
        sq = sb("sq", [P, 2, 2, 256], F32)
        vx = sb("vx", [P, 2, 2, 2, 8, 18], F16)
        extT = sb("extT", [P, 2, 8, 256], F16)
        eq = sb("eq", [P, 2, 2, 1024], F32)
        eq_lo = sb("eq_lo", [P, 2, 2, 1024], F16)
        ek = sb("ek", [P, 2, 2, 1024], F32)
        ek_lo = sb("ek_lo", [P, 2, 2, 1024], F16)
        kvm = sb("kvm", [P, 8, 18], F32)
        kvr = sb("kvr", [P, 8, 18], F32)
        kvp = sb("kvp", [P, 3, 8, 18], BF16)
        den = sb("den", [P, 16, 2], F32)
        rden = sb("rden", [P, 16, 2], F32)
        at_f = sb("at_f", [P, 2, D], F32)
        at_s = sb("at_s", [P, 2, 2, D], F16)
        atT = sb("atT", [P, 2, 256], F16)
        mv2 = sb("mv2", [P, 2, 2, 2], F32)
        x2_f = sb("x2_f", [P, 2, D], F32)
        rows = sb("rows", [P, 2, TOPK, 2, ROW], F16)
        x2T = sb("x2T", [P, 2, 256], F16)
        lg2 = sb("lg2", [P, 2, E], F32)
        cand = sb("cand", [P, 2, 2, 2, E], F32)
        top = sb("top", [P, 4, 2], F32)
        pick = sb("pick", [P, 2, 2, E], F32)
        both = sb("both", [P, 2, 2, E], F16)
        gap = sb("gap", [P, 2, 2], F32)
        cum1 = sb("cum1", [P, E], F16)
        zbias = sb("zbias", [P, 1], F32)
        where = sb("where", [P, 2, E], F32)
        hit = sb("hit", [P, 2, 2, E], F32)
        slot_f = sb("slot_f", [P, 4], F32)
        slot = sb("slot", [P, 2, 4], U32)

        pad = sb("pad", [P, 2, ROW], F16)
        cnt = sb("cnt", [P, E], F32)
        cnt_i = sb("cnt_i", [P, E], I32)
        up_i = sb("up_i", [P, 2, E], I32)
        sums3 = sb("sums3", [P, 4, 4 + E], F32)
        skip = sb("skip", [P, E], F32)
        tnum = sb("tnum", [P, NX], F32)
        past = sb("past", [P, NX, E], F32)
        jump = sb("jump", [P, NX, E], F32)
        tab_f = sb("tab_f", [P, 2, 2, NX], F32)
        tab = sb("tab", [P, 2, NX], I32)

        primed = sb("primed", [P, 1], F32)
        xl = sb("xl", [P, 2, 2, ROW], F16)
        xlT = sb("xlT", [P, 2, 2, SLOTS], F16)
        gate, act_f = (eq[:, k, 0].rearrange("p (k n) -> p k n", k=2) for k in range(2))
        act_hi = sb("act_hi", [P, 2, 4, SLOTS], F16)
        act_lo = sb("act_lo", [P, 2, 4, SLOTS], F16)
        y = sb("y", [P, 2, 2, D], F32)
        row_id = sb("row_id", [P, NX, 2], I32)
        odds1 = sb("odds1", [P, NX, 2], F32)
        coef = sb("coef", [P, NX, 2], F32)
        put_id = sb("put_id", [P, 2, 2], I32)

        z = psum("z", [P, 2, 1024], F32)
        bT = psum("bT", [P, 1024], F16)
        bQ = psum("bQ", [P, 2, 512], F32)
        bM = psum("bM", [P, 512], F32)
        m_out = bM[:, 0:288].rearrange("p (t j c) -> p t j c", t=2, j=8)
        m_kv = bM[:, 288:432].rearrange("p (j c) -> p j c", j=8)
        m_rt = bM[:, 432:448].rearrange("p (t e) -> p t e", t=2)
        m_pos = bM[:, 448:464].rearrange("p (t e) -> p t e", t=2)

        dve_passed, pool_passed = sem("dve_passed"), sem("pool_passed")
        xload = [sem(f"xload{i}") for i in range(2)]
        wload = [sem(f"wload{i}") for i in range(2)]
        cload = sem("cload")
        rload = sem("rload")
        pset = sem("pset")
        wa_hi_set, wa_lo_set, rf_hi_set, rf_set = sem("wa_hi_set"), sem("wa_lo_set"), sem("rf_hi_set"), sem("rf_set")
        wsplit_hi, wsplit_lo = sem("wsplit_hi"), sem("wsplit_lo")
        ln1_st, rs_st = sem("ln1_st"), sem("rs_st")
        xn_set, xnhi_set, xnlo_set, bias_set = sem("xn_set"), sem("xnhi_set"), sem("xnlo_set"), sem("bias_set")
        t_ln1, t_extq, t_extk, t_att, t_ln2 = (sem(n) for n in ("t_ln1", "t_extq", "t_extk", "t_att", "t_ln2"))
        t_read = sem("t_read")
        q_done, q_read, qlo_set, ss_set = (sem(n) for n in ("q_done", "q_read", "qlo_set", "ss_set"))
        v_set, nrm_st, nrm_set = sem("v_set"), sem("nrm_st"), sem("nrm_set")
        z_done, z_exp, eklo_set = sem("z_done"), sem("z_exp"), sem("eklo_set")
        eqlo_set = [sem(f"eqlo_set{i}") for i in range(2)]
        kv_done, kv_st, kv_set = sem("kv_done"), sem("kv_st"), sem("kv_set")
        m_read = sem("m_read")
        o_done, at_st, athi_set, atlo_set = sem("o_done"), sem("at_st"), sem("athi_set"), sem("atlo_set")
        w_done, ln2_st = sem("w_done"), sem("ln2_st")
        x2_set, x2hi_set, x2lo_set, rows_set = sem("x2_set"), sem("x2hi_set"), sem("x2lo_set"), sem("rows_set")
        rt_done, rt_st, both_set, pos_done, slot_set = (
            sem(n) for n in ("rt_done", "rt_st", "both_set", "pos_done", "slot_set"))
        cum_set, cum_st, zb_set = sem("cum_set"), sem("cum_st"), sem("zb_set")
        scat = [sem(f"scat{i}") for i in range(2)]

        cnt_done, ph2, cnt_set, tab_set, tail = (
            sem(n) for n in ("cnt_done", "ph2", "cnt_set", "tab_set", "tail"))
        xl_load = [sem(f"xl_load{i}") for i in range(2)]
        y_scat = [sem(f"y_scat{i}") for i in range(2)]
        id_kept = sem("id_kept")
        xl_turned, xlT_set, h_done, silu_set, act_set, acthi_set, actlo_set, y_done, y_set = (
            sem(n) for n in ("xl_turned", "xlT_set", "h_done", "silu_set", "act_set", "acthi_set", "actlo_set",
                             "y_done", "y_set"))
        tokens_set, eps_set = sem("tokens_set"), sem("eps_set")
        odds_set, odds1_set, coef_set, stored = sem("odds_set"), sem("odds1_set"), sem("coef_set"), sem("stored")

        out_t = out.rearrange("(t p) d -> p t d", p=P)
        bf_hi = lambda a: a.bitcast(BF16).rearrange("p (n two) -> p two n", two=2)[:, 1, :]

        def pad_region(eng, engine, e):
            n = nc.values_load(cnt_i[0:1, e:e + 1], engines=[engine], min_val=0, max_val=T,
                               skip_runtime_bounds_check_because="counts of tokens")
            return eng.dma_start(xs[bass.ds(n + e * CAP, SLOTS), :].rearrange("(h p) r -> p h r", p=P),
                                 pad[:].bitcast(I32))

        with nc.Block() as block:
            @block.sync
            def _(sp):
                sp.dma_start(wa_f[:], wa).then_inc(cload, 16)
                sp.dma_start(b_bc[:], bout).then_inc(cload, 16)
                sp.dma_start(kvmask[:], mask).then_inc(cload, 16)

                def load(b, p):
                    need(sp, xload[p], 8 * (b - p))
                    sp.dma_start(xall[:, bass.ds(b * 2, 2), :], x[:, bass.ds(b * 2, 2), :]).then_inc(xload[p], 16)
                    need(sp, wsplit_lo, b - 1)
                    sp.dma_start(w_st[:, p, :], wffn[:, bass.ds(b * WCH, WCH)]).then_inc(wload[p], 16)

                def store(b, p):
                    sp.wait_ge(q_read, reads_before(BANK_Q, Q_WOUT, b) + 1)
                    sp.dma_start(out_t[:, bass.ds(b * 2, 2), :], xall[:, bass.ds(b * 2, 2), :]).then_inc(stored, 16)

                pipeline(sp, [(0, load), (LAG, store)])

                sp.wait_ge(pset, 16)
                sp.dma_start(xs[E * CAP:E * CAP + SLOTS, :].rearrange("(h p) r -> p h r", p=P),
                             pad[:].bitcast(I32)).then_inc(tail, 16)
                sp.wait_ge(cnt_set, 1)
                for e in range(E // 2):
                    pad_region(sp, mybir.EngineType.SP, e).then_inc(tail, 16)
                sp.wait_ge(tail, 16 * (E + 1))
                sp.wait_ge(tab_set, 1)
                for p in range(2):
                    sp.wait_ge(scat[p], 64 * NB // 2)

                def fetch(t, p):
                    need(sp, xl_turned, t - 1)
                    need(sp, odds1_set, t - 1)
                    r = nc.values_load(tab[0:1, 1, bass.ds(t, 1)], engines=[mybir.EngineType.SP], min_val=0,
                                       max_val=E * CAP, skip_runtime_bounds_check_because="clamped to the last tile")
                    sp.dma_start(xl[:, p].bitcast(I32), xs[bass.ds(r, SLOTS), :].rearrange(
                        "(h p) r -> p h r", p=P)).then_inc(xl_load[p], 16)

                pipeline(sp, [(0, fetch)], 0, NX)

            def landed(b, p):
                return 8 * (b - p) + 16

            @block.gpsimd
            def _(pool):
                nc.gpsimd.memset(ident[:], 0.0).then_inc(pset, 1)
                nc.gpsimd.memset(tri[:], 0.0).then_inc(pset, 1)
                nc.gpsimd.memset(ones[:], 1.0).then_inc(pset, 1)
                nc.gpsimd.memset(mcum[:], 0.0).then_inc(pset, 1)
                nc.gpsimd.memset(vx[:, :, :, 0, :, 16:18], 1.0).then_inc(pset, 1)
                nc.gpsimd.memset(vx[:, :, :, 1, :, 16:18], 0.0).then_inc(pset, 1)
                nc.gpsimd.iota(ids[:], [[P, NT]], base=0, channel_multiplier=1).then_inc(pset, 1)
                nc.gpsimd.iota(rank[:], [[-1, E]], base=E, channel_multiplier=0,
                               allow_small_or_imprecise_dtypes=True).then_inc(pset, 1)
                nc.gpsimd.iota(ebase[:], [[CAP, E]], base=0, channel_multiplier=0,
                               allow_small_or_imprecise_dtypes=True).then_inc(pset, 1)
                nc.gpsimd.iota(tnum[:], [[1, NX]], base=0, channel_multiplier=0,
                               allow_small_or_imprecise_dtypes=True).then_inc(pset, 1)
                nc.gpsimd.memset(pad[:], 0.0).then_inc(pset, 1)
                nc.gpsimd.memset(sums3[:], 0.0).then_inc(pset, 1)
                nc.gpsimd.memset(rs[:, :, 0:2], 1.0).then_inc(pset, 1)
                pool.wait_ge(pset, 13)
                nc.gpsimd.memset(pad[:, :, ID:ID + 2].bitcast(I32), PAD_ID).then_inc(pset, 1)
                nc.gpsimd.affine_select(out=ident[:], in_=ident[:], compare_op=ALU.not_equal, fill=1.0, base=0,
                                        pattern=[[-1, P]], channel_multiplier=1).then_inc(pset, 1)
                nc.gpsimd.affine_select(out=tri[:], in_=tri[:], compare_op=ALU.is_ge, fill=1.0, base=0,
                                        pattern=[[-1, P]], channel_multiplier=1).then_inc(pset, 1)

                def roots(it, q):
                    a, y, t, e = (rs[:, q, k] for k in range(4))
                    if isinstance(it, int) and it < min(R_LN1, R_NORM, R_LN2):
                        nc.gpsimd.memset(e, 1.0).then_inc(rs_st, RS)
                        return
                    if isinstance(it, int) and it >= NB + max(R_LN1, R_NORM, R_LN2):
                        return
                    need(pool, xn_set, 2 * batches(it - 2, R_LN1))
                    need(pool, x2_set, 2 * batches(it - 2, R_LN2))
                    need(pool, nrm_set, batches(it - 2, R_NORM))
                    need(pool, ss_set, batches(it, R_NORM))
                    need(pool, rs_st, (it - 1) * RS)
                    for lag, mv, st, c in ((R_LN2, mv2, ln2_st, 66), (R_LN1, mv1, ln1_st, 64)):
                        if not isinstance(it, int) or 0 <= it - lag < NB:
                            wait_apart(pool, pool_passed, st, 4 * batches(it, lag))
                            nc.gpsimd.tensor_scalar(rs[:, q, 0, c:c + 2], mv[:, (q + lag) % 2, :, 1], LN_EPS, None,
                                                    ALU.add).then_inc(eps_set, 1)
                    wait_apart(pool, pool_passed, eps_set, batches(it, R_LN2) + batches(it, R_LN1))
                    nc.gpsimd.tensor_scalar(y.bitcast(I32), a.bitcast(I32), -0.5, GUESS, ALU.mult,
                                            ALU.add).then_inc(rs_st, 1)
                    pool.wait_ge(rs_st, it * RS + 1)
                    nc.gpsimd.tensor_tensor(out=t, in0=a, in1=y, op=ALU.mult).then_inc(rs_st, 1)
                    pool.wait_ge(rs_st, it * RS + 2)
                    nc.gpsimd.tensor_tensor(out=e, in0=t, in1=y, op=ALU.mult).then_inc(rs_st, 1)
                    wait_apart(pool, pool_passed, rs_st, it * RS + 3)
                    nc.gpsimd.tensor_scalar(t, e, 0.375, -1.25, ALU.mult, ALU.add).then_inc(rs_st, 1)
                    pool.wait_ge(rs_st, it * RS + 4)
                    nc.gpsimd.tensor_tensor(out=t, in0=t, in1=e, op=ALU.mult).then_inc(rs_st, 1)
                    wait_apart(pool, pool_passed, rs_st, it * RS + 5)
                    nc.gpsimd.tensor_scalar(t, t, 1.875, None, ALU.add).then_inc(rs_st, 1)
                    pool.wait_ge(rs_st, it * RS + 6)
                    nc.gpsimd.tensor_tensor(out=y, in0=y, in1=t, op=ALU.mult).then_inc(rs_st, 1)
                    pool.wait_ge(rs_st, it * RS + 7)
                    nc.gpsimd.tensor_tensor(out=t, in0=a, in1=y, op=ALU.mult).then_inc(rs_st, 1)
                    pool.wait_ge(rs_st, it * RS + 8)
                    nc.gpsimd.tensor_tensor(out=e, in0=t, in1=y, op=ALU.mult).then_inc(rs_st, 1)
                    wait_apart(pool, pool_passed, rs_st, it * RS + 9)
                    nc.gpsimd.tensor_scalar(e, e, -0.5, 1.5, ALU.mult, ALU.add).then_inc(rs_st, 1)
                    pool.wait_ge(rs_st, it * RS + 10)
                    nc.gpsimd.tensor_tensor(out=y, in0=y, in1=e, op=ALU.mult).then_inc(rs_st, 1)

                def norms(b, p):
                    q = (p + R_NORM) % 2
                    need(pool, nrm_set, b - 1)
                    pool.wait_ge(rs_st, (b + R_NORM + 1) * RS)
                    nc.gpsimd.tensor_tensor(out=rs[:, q, 4, 0:64], in0=rs[:, q, 0, 0:64], in1=rs[:, q, 1, 0:64],
                                            op=ALU.mult).then_inc(nrm_st, 1)
                    need(pool, t_extk, b - 1)
                    wait_apart(pool, pool_passed, nrm_st, b * 2 + 1)
                    e = ext[:, p].rearrange("p t g c -> p (t g) c")
                    nv = rs[:, q, 4, 0:64].rearrange("p (tg h) -> p tg h", h=4)
                    nc.gpsimd.tensor_copy(e[:, :, 96:100], nv).then_inc(nrm_st, 1)
                    pool.wait_ge(nrm_st, b * 2 + 2)
                    nc.gpsimd.tensor_tensor(out=e[:, :, 100:104], in0=nv, in1=e[:, :, 96:100],
                                            op=ALU.subtract).then_inc(nrm_set, 1)

                def bias(b, p):
                    pool.wait_ge(xn_set, 2 * (b + 1))
                    v = xall[:, bass.ds(b * 2, 2), :]
                    nc.gpsimd.tensor_tensor(out=v, in0=v, in1=b_bc[:].unsqueeze(1).to_broadcast([P, 2, D]),
                                            op=ALU.add).then_inc(bias_set, 1)

                def q_lo(b, p):
                    pool.wait_ge(z_exp, 4 * b + 1)
                    need(pool, o_done, b - 1)
                    nc.gpsimd.tensor_tensor(out=eq_lo[:, p, 0], in0=eq[:, p, 0], in1=bf_hi(eq[:, p, 0]),
                                            op=ALU.subtract).then_inc(eqlo_set[0], 1)

                def w_part(b, p):
                    wait_apart(pool, pool_passed, wsplit_hi, 2 * (b + 1))
                    w = bass.ds(b * WCH, WCH)
                    nc.gpsimd.tensor_tensor(out=w_lo[:, w], in0=w_st[:, p, :], in1=w_hi[:, w],
                                            op=ALU.subtract).then_inc(wsplit_lo, 1)

                def tokens(b, p):
                    need(pool, tokens_set, b - 1)
                    wait_apart(pool, pool_passed, scat[p], 32 * (b - p))
                    nc.gpsimd.tensor_copy(rows[:, p, :, :, ID:ID + 2].bitcast(I32), ids[:, bass.ds(b * 2, 2)].unsqueeze(
                        1).unsqueeze(3).to_broadcast([P, TOPK, 2, 1])).then_inc(tokens_set, 1)

                def scatter(b, p):
                    pool.wait_ge(slot_set, b + 1)
                    pool.wait_ge(odds_set, 2 * (b + 1))
                    pool.wait_ge(tokens_set, b + 1)
                    wait_apart(pool, pool_passed, rows_set, b + 1)
                    for k in range(TOPK):
                        for t in range(2):
                            pool.indirect_dma_start(
                                out=xs[:, :], out_offset=bass.IndirectOffsetOnAxis(
                                    ap=slot[:, p, 2 * k + t:2 * k + t + 1], axis=0),
                                in_=rows[:, p, k, t, :].bitcast(I32), in_offset=None).then_inc(scat[p], 16)

                pool.wait_ge(cload, 48)
                pipeline(pool, [(None, roots), (2, norms), (3, bias), (5, scatter), (2, q_lo), (0, w_part),
                                (3, tokens)])

                def put(t, p):
                    pool.wait_ge(y_set, 3 * (t + 1))
                    wait_apart(pool, pool_passed, y_scat[1 - p], 16 * (t + p))
                    for h in range(2):
                        pool.indirect_dma_start(
                            out=out[:, :], out_offset=bass.IndirectOffsetOnAxis(
                                ap=put_id[:, p, h:h + 1].bitcast(U32), axis=0),
                            in_=y[:, p, h, :], in_offset=None, bounds_check=T - 1,
                            oob_is_err=False, compute_op=ALU.add).then_inc(y_scat[p], 16)

                pool.wait_ge(tail, 16 * (E + 1))
                pool.wait_ge(stored, 16 * NB)
                pipeline(pool, [(2, put)], 2, NX)
                for p in range(2):
                    pool.wait_ge(y_scat[p], 32 * NX // 2)

            @block.scalar
            def _(act):
                act.dma_start(rf_f[:], features_w).then_inc(rload, 16)
                act.wait_ge(rload, 16)
                nc.scalar.activation(rf[:], rf_f[:], ACT.Copy).then_inc(rf_hi_set, 1)
                act.wait_ge(cload, 48)
                nc.scalar.activation(wa_hi[:], wa_f[:], ACT.Copy, scale=W_SCALE).then_inc(wa_hi_set, 1)

                def xn_hi(b, p):
                    act.wait_ge(xn_set, 2 * (b + 1))
                    need(act, t_ln1, b - 1)
                    nc.scalar.activation(xn_s[:, p, 0], xn_f[:, p], ACT.Copy).then_inc(xnhi_set, 1)

                def xt_copy(b, p):
                    act.wait_ge(t_ln1, b + 1)
                    need(act, q_done, 2 * (b - 1))
                    nc.scalar.activation(xT[:, p].rearrange("p a n -> p (a n)"), bT[:, 0:512],
                                         ACT.Copy).then_inc(t_read, 1)

                def qkv_hi(t):
                    def stage(b, p):
                        act.wait_ge(q_done, 2 * b + t + 1)
                        if t == 0:
                            need(act, t_extk, b - 1)
                            need(act, kv_done, b - 1)
                            need(act, ss_set, b - 1)
                        qk = bQ[:, t, 0:256]
                        nc.scalar.activation(
                            ext[:, p, t].rearrange("p g (s c) -> p g s c", s=2)[:, :, :, 0:32],
                            qk.rearrange("p (g c) -> p g c", g=8).unsqueeze(2).to_broadcast([P, 8, 2, 32]),
                            ACT.Copy)
                        nc.scalar.activation(sq[:, p, t, :], qk, ACT.Square)
                        nc.scalar.activation(vx[:, p, t, 0, :, 0:16],
                                             bQ[:, t, 256:384].rearrange("p (j c) -> p j c", j=8),
                                             ACT.Copy).then_inc(v_set, 1)
                    return stage

                def ext_copy(half, done):
                    def stage(b, p):
                        act.wait_ge(done, b + 1)
                        if half == 0:
                            need(act, z_done, 4 * (b - 1))
                        nc.scalar.activation(extT[:, p, 4 * half:4 * half + 4, :].rearrange("p g n -> p (g n)"),
                                             bT[:], ACT.Copy).then_inc(t_read, 1)
                    return stage

                def exp(k):
                    def stage(b, p):
                        act.wait_ge(z_done, 4 * b + k + 1)
                        if k < 2:
                            need(act, o_done, b - 1)
                            need(act, eqlo_set[k], b - 1)
                            dst = eq[:, p, k]
                        else:
                            need(act, kv_done, b - 1)
                            dst = ek[:, p, k - 2]
                        nc.scalar.activation(dst, z[:, k % 2], ACT.Exp, bias=zbias[:, 0:1],
                                             scale=1.0 / (8 * W_SCALE)).then_inc(z_exp, 1)
                    return stage

                def att_hi(b, p):
                    act.wait_ge(m_read, reads_before(BANK_M, M_OUT, b) + 1)
                    need(act, t_att, b)
                    nc.scalar.activation(at_s[:, 0], at_f[:], ACT.Copy).then_inc(athi_set, 1)

                def att_copy(b, p):
                    act.wait_ge(t_att, b + 1)
                    need(act, w_done, b)
                    nc.scalar.activation(atT[:].rearrange("p a n -> p (a n)"), bT[:, 0:512],
                                         ACT.Copy).then_inc(t_read, 1)

                def x2_hi(b, p):
                    act.wait_ge(x2_set, 2 * (b + 1))
                    need(act, scat[p], 32 * (b - p))
                    need(act, rows_set, b - 1)
                    nc.scalar.activation(rows[:, p, 0, :, 0:D], x2_f[:], ACT.Copy).then_inc(x2hi_set, 1)

                def x2_copy(b, p):
                    act.wait_ge(t_ln2, b + 1)
                    need(act, rt_done, b)
                    nc.scalar.activation(x2T[:].rearrange("p a n -> p (a n)"), bT[:, 0:512],
                                         ACT.Copy).then_inc(t_read, 1)

                def second_rows(b, p):
                    act.wait_ge(x2lo_set, b + 1)
                    need(act, scat[p], 32 * (b - p))
                    nc.scalar.activation(rows[:, p, 1, :, 0:2 * D], rows[:, p, 0, :, 0:2 * D],
                                         ACT.Copy).then_inc(rows_set, 1)

                def odds(b, p):
                    act.wait_ge(rt_st, b * 13 + 11)
                    need(act, scat[p], 32 * (b - p))
                    for k in range(TOPK):
                        nc.scalar.activation(rows[:, p, k, :, ODDS:ODDS + 2].bitcast(F32), gap[:, p].unsqueeze(2),
                                             ACT.Exp, scale=(1 - 2 * k) / W_SCALE).then_inc(odds_set, 1)

                def w_part(b, p):
                    act.wait_ge(wload[p], landed(b, p))
                    nc.scalar.activation(w_hi[:, bass.ds(b * WCH, WCH)], w_st[:, p, :], ACT.Copy,
                                         scale=W_SCALE).then_inc(wsplit_hi, 1)
                    act.wait_ge(wsplit_hi, 2 * b + 1)
                    nc.scalar.activation(w_st[:, p, :], w_st[:, p, :], ACT.Copy, scale=W_SCALE).then_inc(wsplit_hi, 1)

                act.wait_ge(zb_set, 1)
                pipeline(act, [(0, w_part), (4, x2_hi), (2, ext_copy(0, t_extq)), (3, att_hi), (4, x2_copy),
                               (4, second_rows), (3, att_copy), (2, exp(0)), (2, ext_copy(1, t_extk)), (2, exp(1)),
                               (1, xt_copy), (2, exp(2)), (1, qkv_hi(0)), (1, qkv_hi(1)), (2, exp(3)), (4, odds),
                               (0, xn_hi)])

                def silu(k):
                    def stage(t, p):
                        act.wait_ge(h_done, 2 * t + k + 1)
                        need(act, act_set, 2 * t + k - 1)
                        nc.scalar.activation(gate[:, k].rearrange("p (b n) -> p b n", b=2), z[:, k].rearrange(
                            "p (b w n) -> p b w n", b=2, w=2)[:, :, 0, :], ACT.Silu,
                            scale=1.0 / W_SCALE).then_inc(silu_set, 1)
                    return stage

                def act_high(k):
                    def stage(t, p):
                        act.wait_ge(act_set, 2 * t + k + 1)
                        need(act, y_done, t - 1)
                        nc.scalar.activation(act_hi[:, p, 2 * k:2 * k + 2].rearrange("p b n -> p (b n)"),
                                             act_f[:, k], ACT.Copy).then_inc(acthi_set, 1)
                    return stage

                act.wait_ge(cnt_set, 1)
                for e in range(E // 2, E):
                    pad_region(act, mybir.EngineType.Activation, e).then_inc(tail, 16)
                nc.scalar.activation(primed[:], zbias[:], ACT.Silu)
                pipeline(act, [(1, silu(0)), (1, silu(1)), (1, act_high(0)), (1, act_high(1))], 2, NX)

            @block.vector
            def _(dve):
                nc.vector.memset(zbias[:], Z_LN).then_inc(zb_set, 1)
                nc.vector.memset(ext[:], 0.0).then_inc(zb_set, 1)
                nc.vector.memset(rows[:], 0.0).then_inc(zb_set, 1)
                dve.wait_ge(rf_hi_set, 1)
                nc.vector.tensor_tensor(out=rf[64:96, :], in0=rf_f[64:96, :], in1=rf[64:96, :],
                                        op=ALU.subtract).then_inc(rf_set, 1)
                dve.wait_ge(wa_hi_set, 1)
                nc.vector.scalar_tensor_tensor(out=wa_lo[:], in0=wa_f[:], scalar=W_SCALE, in1=wa_hi[:],
                                               op0=ALU.mult, op1=ALU.subtract).then_inc(wa_lo_set, 1)
                dve.wait_ge(pset, 16)

                def stats(b, p, k, mv, st, base):
                    for t in range(2):
                        nc.vector.bn_stats(bn[:, k, t, :], xall[:, bass.ds(b * 2 + t, 1), :].rearrange(
                            "p o d -> p (o d)")).then_inc(st, 1)
                    for t in range(2):
                        wait_apart(dve, dve_passed, st, base + t + 1)
                        nc.vector.bn_aggr(mv[:, p, t, :], bn[:, k, t, :]).then_inc(st, 1)

                def ln1_stats(b, p):
                    dve.wait_ge(xload[p], landed(b, p))
                    need(dve, rs_st, (b + (R_LN1 - 1)) * RS)
                    wait_apart(dve, dve_passed, xn_set, 2 * (b - 1))
                    stats(b, p, 0, mv1, ln1_st, 4 * b)

                def ln_1(b, p):
                    dve.wait_ge(rs_st, (b + R_LN1 + 1) * RS)
                    need(dve, xnhi_set, b - 1)
                    need(dve, xnlo_set, b - 1)
                    for t in range(2):
                        nc.vector.tensor_scalar(xn_f[:, p, t, :], xall[:, bass.ds(b * 2 + t, 1), :].rearrange(
                            "p o d -> p (o d)"), mv1[:, p, t, 0:1], rs[:, (p + R_LN1) % 2, 1, 64 + t:65 + t],
                            ALU.subtract, ALU.mult).then_inc(xn_set, 1)

                def ln1_lo(b, p):
                    dve.wait_ge(xnhi_set, b + 1)
                    dve.wait_ge(xn_set, 2 * (b + 1))
                    nc.vector.tensor_tensor(out=xn_s[:, p, 1], in0=xn_f[:, p], in1=xn_s[:, p, 0],
                                            op=ALU.subtract).then_inc(xnlo_set, 1)

                def split(b, p):
                    dve.wait_ge(v_set, 2 * (b + 1))
                    e = ext[:, p]
                    nc.vector.tensor_tensor(out=e[:, :, :, 32:64], in0=bQ[:, :, 0:256].rearrange(
                        "p t (g c) -> p t g c", g=8), in1=e[:, :, :, 0:32], op=ALU.subtract).then_inc(qlo_set, 1)
                    nc.vector.tensor_tensor(
                        out=vx[:, p, :, 1, :, 0:16], in0=bQ[:, :, 256:384].rearrange("p t (j c) -> p t j c", j=8),
                        in1=vx[:, p, :, 0, :, 0:16], op=ALU.subtract).then_inc(q_read, 1)

                def sums(b, p):
                    dve.wait_ge(v_set, 2 * (b + 1))
                    need(dve, rs_st, (b + (R_NORM - 1)) * RS)
                    need(dve, nrm_st, b * 2 - 3)
                    nc.vector.tensor_reduce(rs[:, (p + R_NORM) % 2, 0, 0:64],
                                            sq[:, p].rearrange("p t (h d) -> p (t h) d", d=HD),
                                            AX.X, ALU.add).then_inc(ss_set, 1)

                def exp_lo(k):
                    def stage(b, p):
                        dve.wait_ge(z_exp, 4 * b + k + 1)
                        if k < 2:
                            src, dst, done = eq[:, p, k], eq_lo[:, p, k], eqlo_set[1]
                            need(dve, o_done, b - 1)
                        else:
                            src, dst, done = ek[:, p, k - 2], ek_lo[:, p, k - 2], eklo_set
                            need(dve, kv_done, b - 1)
                        nc.vector.tensor_tensor(out=dst, in0=src, in1=bf_hi(src), op=ALU.subtract).then_inc(done, 1)
                    return stage

                def kv_parts(b, p):
                    dve.wait_ge(kv_done, b + 1)
                    need(dve, o_done, b)
                    need(dve, kv_st, 3 * b)
                    nc.vector.tensor_tensor(out=kvm[:], in0=m_kv, in1=kvmask[:].unsqueeze(1).to_broadcast([P, 8, 18]),
                                            op=ALU.mult).then_inc(m_read, 1)
                    dve.wait_ge(m_read, reads_before(BANK_M, M_KV, b) + 1)
                    nc.vector.tensor_copy(kvp[:, 0], kvm[:]).then_inc(kv_st, 1)
                    dve.wait_ge(kv_st, 3 * b + 1)
                    nc.vector.tensor_tensor(out=kvr[:], in0=kvm[:], in1=kvp[:, 0],
                                            op=ALU.subtract).then_inc(kv_st, 1)
                    dve.wait_ge(kv_st, 3 * b + 2)
                    nc.vector.tensor_copy(kvp[:, 1], kvr[:]).then_inc(kv_st, 1)
                    dve.wait_ge(kv_st, 3 * b + 3)
                    nc.vector.tensor_tensor(out=kvp[:, 2], in0=kvr[:], in1=kvp[:, 1],
                                            op=ALU.subtract).then_inc(kv_set, 1)

                def divide(b, p):
                    need(dve, athi_set, b)
                    need(dve, atlo_set, b)
                    need(dve, at_st, 2 * b)
                    dve.wait_ge(o_done, b + 1)
                    o = m_out.rearrange("p t j c -> p (t j) c")
                    nc.vector.tensor_scalar(den[:], o[:, :, 16:18], 1e-6 * Z2, None, ALU.add).then_inc(at_st, 1)
                    dve.wait_ge(at_st, 2 * b + 1)
                    nc.vector.reciprocal(rden[:], den[:]).then_inc(at_st, 1)
                    dve.wait_ge(at_st, 2 * b + 2)
                    nc.vector.tensor_tensor(
                        out=at_f[:].rearrange("p t (j h c) -> p (t j) h c", j=8, h=2),
                        in0=o[:, :, 0:16].rearrange("p j (h c) -> p j h c", h=2),
                        in1=rden[:].unsqueeze(3).to_broadcast([P, 16, 2, 8]), op=ALU.mult).then_inc(m_read, 1)

                def att_lo(b, p):
                    dve.wait_ge(athi_set, b + 1)
                    dve.wait_ge(m_read, reads_before(BANK_M, M_OUT, b) + 1)
                    nc.vector.tensor_tensor(out=at_s[:, 1], in0=at_f[:], in1=at_s[:, 0],
                                            op=ALU.subtract).then_inc(atlo_set, 1)

                def residual(b, p):
                    dve.wait_ge(bias_set, b + 1)
                    dve.wait_ge(w_done, b + 1)
                    v = xall[:, bass.ds(b * 2, 2), :]
                    nc.vector.scalar_tensor_tensor(out=v, in0=bQ[:, :, 384:512], scalar=1.0 / (W_SCALE * W_SCALE),
                                                   in1=v, op0=ALU.mult, op1=ALU.add).then_inc(q_read, 1)

                def ln2_stats(b, p):
                    dve.wait_ge(q_read, reads_before(BANK_Q, Q_WOUT, b) + 1)
                    need(dve, rs_st, (b + (R_LN2 - 1)) * RS)
                    wait_apart(dve, dve_passed, x2_set, 2 * (b - 1))
                    stats(b, p, 1, mv2, ln2_st, 4 * b)

                def ln_2(b, p):
                    dve.wait_ge(rs_st, (b + R_LN2 + 1) * RS)
                    need(dve, x2hi_set, b)
                    need(dve, x2lo_set, b)
                    for t in range(2):
                        nc.vector.tensor_scalar(x2_f[:, t, :], xall[:, bass.ds(b * 2 + t, 1), :].rearrange(
                            "p o d -> p (o d)"), mv2[:, p, t, 0:1], rs[:, (p + R_LN2) % 2, 1, 66 + t:67 + t],
                            ALU.subtract, ALU.mult).then_inc(x2_set, 1)

                def ln2_lo(b, p):
                    dve.wait_ge(x2hi_set, b + 1)
                    dve.wait_ge(x2_set, 2 * (b + 1))
                    nc.vector.tensor_tensor(out=rows[:, p, 0, :, D:2 * D], in0=x2_f[:], in1=rows[:, p, 0, :, 0:D],
                                            op=ALU.subtract).then_inc(x2lo_set, 1)

                def route_a(b, p):
                    n = 13 * b
                    bc = lambda a: a.unsqueeze(2).to_broadcast([P, 2, E])
                    rk = rank[:].unsqueeze(1).to_broadcast([P, 2, E])
                    dve.wait_ge(rt_done, b + 1)
                    need(dve, rt_st, n)
                    src = m_rt
                    for k in range(2):
                        nc.vector.tensor_reduce(top[:, k], src, AX.X, ALU.max).then_inc(rt_st, 1)
                        dve.wait_ge(rt_st, n + 5 * k + 1)
                        nc.vector.tensor_tensor(out=cand[:, k, 0], in0=src, in1=bc(top[:, k]),
                                                op=ALU.is_equal).then_inc(rt_st, 1)
                        dve.wait_ge(rt_st, n + 5 * k + 2)
                        nc.vector.tensor_tensor(out=cand[:, k, 1], in0=cand[:, k, 0], in1=rk,
                                                op=ALU.mult).then_inc(rt_st, 1)
                        dve.wait_ge(rt_st, n + 5 * k + 3)
                        nc.vector.tensor_reduce(top[:, 2 + k], cand[:, k, 1], AX.X, ALU.max).then_inc(rt_st, 1)
                        dve.wait_ge(rt_st, n + 5 * k + 4)
                        nc.vector.tensor_tensor(out=pick[:, k], in0=cand[:, k, 1], in1=bc(top[:, 2 + k]),
                                                op=ALU.is_equal).then_inc(rt_st, 1)
                        dve.wait_ge(rt_st, n + 5 * k + 5)
                        if k == 0:
                            nc.vector.scalar_tensor_tensor(out=lg2[:], in0=pick[:, 0], scalar=-3.0e38, in1=m_rt,
                                                           op0=ALU.mult, op1=ALU.add).then_inc(m_read, 1)
                            dve.wait_ge(m_read, reads_before(BANK_M, M_RT, b) + 1)
                            src = lg2[:]
                    need(dve, odds_set, 2 * (b - 1))
                    nc.vector.tensor_tensor(out=gap[:, p], in0=top[:, 1], in1=top[:, 0],
                                            op=ALU.subtract).then_inc(rt_st, 1)
                    need(dve, pos_done, b - 1)
                    nc.vector.tensor_tensor(out=both[:, p], in0=pick[:, 0], in1=pick[:, 1],
                                            op=ALU.add).then_inc(both_set, 1)

                def route_b(b, p):
                    dve.wait_ge(pos_done, b + 1)
                    nc.vector.tensor_tensor(out=where[:], in0=m_pos, in1=ebase[:].unsqueeze(1).to_broadcast([P, 2, E]),
                                            op=ALU.add).then_inc(m_read, 1)
                    nc.vector.tensor_tensor(out=cum1[:], in0=mcum[:], in1=both[:, p, 0], op=ALU.add).then_inc(cum_st, 1)
                    dve.wait_ge(m_read, reads_before(BANK_M, M_POS, b) + 1)
                    nc.vector.tensor_tensor(out=hit[:], in0=pick[:], in1=where[:].unsqueeze(1).to_broadcast(
                        [P, TOPK, 2, E]), op=ALU.mult).then_inc(rt_st, 1)
                    dve.wait_ge(cum_st, b + 1)
                    nc.vector.tensor_tensor(out=mcum[:], in0=cum1[:], in1=both[:, p, 1],
                                            op=ALU.add).then_inc(cum_set, 1)
                    dve.wait_ge(rt_st, 13 * b + 12)
                    nc.vector.tensor_reduce(slot_f[:], hit[:].rearrange("p k t e -> p (k t) e"), AX.X,
                                            ALU.add).then_inc(rt_st, 1)
                    dve.wait_ge(rt_st, 13 * b + 13)
                    need(dve, scat[p], 32 * (b - p))
                    nc.vector.tensor_copy(slot[:, p], slot_f[:]).then_inc(slot_set, 1)

                pipeline(dve, [(4, ln_2), (3, divide), (4, ln2_lo), (0, ln1_stats), (3, att_lo), (4, route_a),
                               (3, residual), (3, ln2_stats), (2, exp_lo(2)), (1, sums), (2, exp_lo(3)),
                               (2, exp_lo(1)), (2, kv_parts), (4, route_b), (0, ln_1), (1, split), (0, ln1_lo)])

                n = [0]

                def chain(ins):
                    n[0] += 1
                    ins.then_inc(ph2, 1)
                    dve.wait_ge(ph2, n[0])

                dve.wait_ge(cnt_done, 1)
                chain(nc.vector.tensor_copy(cnt[:], bM[:, 0:E]))
                nc.vector.tensor_copy(cnt_i[:], cnt[:]).then_inc(cnt_set, 1)
                chain(nc.vector.tensor_scalar(up_i[:, 0], cnt[:], float(SLOTS - 1), None, ALU.add))
                chain(nc.vector.tensor_scalar(up_i[:, 1], up_i[:, 0], SLOTS.bit_length() - 1, None,
                                              ALU.logical_shift_right))
                ntile, ends = sums3[:, 0, 4:], sums3[:, 3, 4:]
                chain(nc.vector.tensor_copy(ntile, up_i[:, 1]))
                for k in range(3):
                    chain(nc.vector.tensor_tensor(out=sums3[:, k + 1, 4:], in0=sums3[:, k, 4:],
                                                  in1=sums3[:, k, 4 - 2 ** k:4 + E - 2 ** k], op=ALU.add))
                chain(nc.vector.tensor_scalar(skip[:], ntile, -float(SLOTS), float(CAP), ALU.mult, ALU.add))
                chain(nc.vector.tensor_tensor(out=past[:], in0=tnum[:].unsqueeze(2).to_broadcast([P, NX, E]),
                                              in1=ends.unsqueeze(1).to_broadcast([P, NX, E]), op=ALU.is_ge))
                chain(nc.vector.tensor_tensor(out=jump[:], in0=past[:], in1=skip[:].unsqueeze(1).to_broadcast(
                    [P, NX, E]), op=ALU.mult))
                chain(nc.vector.tensor_reduce(tab_f[:, 0, 0], past[:], AX.X, ALU.add))
                chain(nc.vector.tensor_reduce(tab_f[:, 0, 1], jump[:], AX.X, ALU.add))
                chain(nc.vector.scalar_tensor_tensor(out=tab_f[:, 1, 1], in0=tnum[:], scalar=float(SLOTS),
                                                     in1=tab_f[:, 0, 1], op0=ALU.mult, op1=ALU.add))
                chain(nc.vector.tensor_scalar(tab[:, 0], tab_f[:, 0, 0], float(E - 1), None, ALU.min))
                nc.vector.tensor_scalar(tab[:, 1], tab_f[:, 1, 1], float(E * CAP), None, ALU.min).then_inc(tab_set, 1)

                def xl_copy(t, p):
                    dve.wait_ge(xl_turned, t + 1)
                    need(dve, h_done, 2 * (t - 1))
                    nc.vector.tensor_copy(xlT[:, p].rearrange("p a n -> p (a n)"), bT[:, 0:512]).then_inc(xlT_set, 1)
                    dve.wait_ge(xl_load[p], 8 * (t - p) + 16)
                    nc.vector.tensor_copy(row_id[:, bass.ds(t, 1), :].unsqueeze(3),
                                          xl[:, p, :, ID:ID + 2].bitcast(I32).unsqueeze(1)).then_inc(id_kept, 1)
                    nc.vector.tensor_scalar(odds1[:, bass.ds(t, 1), :].unsqueeze(3),
                                            xl[:, p, :, ODDS:ODDS + 2].bitcast(F32).unsqueeze(1), 1.0,
                                            W_SCALE * W_SCALE, ALU.add, ALU.mult).then_inc(odds1_set, 1)
                    dve.wait_ge(odds1_set, t + 1)
                    nc.vector.reciprocal(coef[:, bass.ds(t, 1), :], odds1[:, bass.ds(t, 1), :]).then_inc(coef_set, 1)

                def gated(k):
                    def stage(t, p):
                        dve.wait_ge(silu_set, 2 * t + k + 1)
                        need(dve, acthi_set, 2 * t + k - 1)
                        need(dve, actlo_set, 2 * t + k - 1)
                        nc.vector.tensor_tensor(out=act_f[:, k].rearrange("p (b n) -> p b n", b=2),
                                                in0=z[:, k].rearrange("p (b w n) -> p b w n", b=2, w=2)[:, :, 1, :],
                                                in1=gate[:, k].rearrange("p (b n) -> p b n", b=2),
                                                op=ALU.mult).then_inc(act_set, 1)
                    return stage

                def act_low(k):
                    def stage(t, p):
                        dve.wait_ge(acthi_set, 2 * t + k + 1)
                        nc.vector.tensor_tensor(
                            out=act_lo[:, p, 2 * k:2 * k + 2].rearrange("p b n -> p (b n)"), in0=act_f[:, k],
                            in1=act_hi[:, p, 2 * k:2 * k + 2].rearrange("p b n -> p (b n)"),
                            op=ALU.subtract).then_inc(actlo_set, 1)
                    return stage

                def y_copy(t, p):
                    dve.wait_ge(y_done, t + 1)
                    need(dve, y_scat[p], 16 * (t - p))
                    dve.wait_ge(coef_set, t + 1)
                    for h in range(2):
                        nc.vector.tensor_scalar(y[:, p, h, :], bQ[:, p, P * h:P * h + P], coef[:, bass.ds(t, 1), h],
                                                None, ALU.mult).then_inc(y_set, 1)
                    dve.wait_ge(id_kept, t + 1)
                    nc.vector.tensor_copy(put_id[:, p, :].unsqueeze(1), row_id[:, bass.ds(t, 1), :]).then_inc(y_set, 1)

                pipeline(dve, [(1, gated(0)), (0, xl_copy), (1, gated(1)), (1, act_low(0)), (1, act_low(1)),
                               (2, y_copy)], 2, NX)

            @block.tensor
            def _(pe):
                mm = nc.tensor.matmul
                pe.wait_ge(pset, 16)
                pe.wait_ge(wa_lo_set, 1)
                pe.wait_ge(rf_set, 1)

                def free_bank(s, bank, k, b):
                    need(pe, s, reads_before(bank, k, b))

                def three(out_, hi, lo, w_h, w_l, start):
                    mm(out_, hi, w_h, start=start, stop=False, skip_group_check=True)
                    mm(out_, hi, w_l, start=False, stop=False, skip_group_check=True)
                    return mm(out_, lo, w_h, start=False, stop=True, skip_group_check=True)

                def turn(src, n):
                    for k in range(n):
                        last = nc.tensor.transpose(bT[:, P * k:P * k + P], src(k), ident[:])
                    return last

                def ext_turn(half, k, done):
                    def stage(b, p):
                        pe.wait_ge(nrm_set, b + 1)
                        pe.wait_ge(qlo_set, b + 1)
                        free_bank(t_read, BANK_T, k, b)
                        turn(lambda n: ext[:, p, n % 2, 4 * half + n // 2, :], 8).then_inc(done, 1)
                    return stage

                def ln1_turn(b, p):
                    pe.wait_ge(xnlo_set, b + 1)
                    free_bank(t_read, BANK_T, T_LN1, b)
                    turn(lambda n: xn_s[:, p, n // 2, n % 2, :], 4).then_inc(t_ln1, 1)

                def att_turn(b, p):
                    pe.wait_ge(atlo_set, b + 1)
                    free_bank(t_read, BANK_T, T_ATT, b)
                    turn(lambda n: at_s[:, n // 2, n % 2, :], 4).then_inc(t_att, 1)

                def ln2_turn(b, p):
                    pe.wait_ge(x2lo_set, b + 1)
                    free_bank(t_read, BANK_T, T_LN2, b)
                    turn(lambda n: rows[:, p, 0, n % 2, D * (n // 2):D * (n // 2) + D], 4).then_inc(t_ln2, 1)

                def qkv(b, p):
                    pe.wait_ge(t_read, reads_before(BANK_T, T_LN1, b) + 1)
                    free_bank(q_read, BANK_Q, Q_QKV, b)
                    for t in range(2):
                        c = slice(P * t, P * t + P)
                        three(bQ[:, t, 0:384], xT[:, p, 0, c], xT[:, p, 1, c], wa_hi[:, 0:384], wa_lo[:, 0:384],
                              True).then_inc(q_done, 1)

                def features(k):
                    def stage(b, p):
                        pe.wait_ge(t_read, reads_before(BANK_T, T_EXTQ if k < 2 else T_EXTK, b) + 1)
                        need(pe, z_exp, 4 * b + k - 1)
                        for n in range(4):
                            o = z[:, k % 2, 256 * n:256 * n + 256]
                            if k < 2:
                                last = mm(o, rf[:, P * (n % 2):P * (n % 2) + P], extT[:, p, 2 * k + n // 2, :],
                                          start=True, stop=True, skip_group_check=True)
                            else:
                                last = mm(o, extT[:, p, 4 + n, P * (k - 2):P * (k - 1)], rf[:], start=True, stop=True,
                                          skip_group_check=True)
                        last.then_inc(z_done, 1)
                    return stage

                def kv(b, p):
                    free_bank(m_read, BANK_M, M_KV, b)
                    pe.wait_ge(q_read, reads_before(BANK_Q, Q_QKV, b) + 1)
                    for t in range(2):
                        pe.wait_ge(eklo_set, 2 * b + t + 1)
                        for j in range(8):
                            f = slice(P * j, P * j + P)
                            for e, c in ((bf_hi(ek[:, p, t, f]), 0), (bf_hi(ek[:, p, t, f]), 1), (ek_lo[:, p, t, f], 0),
                                         (ek_lo[:, p, t, f], 1)):
                                first = t == 0 and j == 0 and c == 0 and e.dtype == BF16
                                last = mm(m_kv[:, j, :], e, vx[:, p, t, c, j, :], start=first, stop=False,
                                          skip_group_check=True)
                    last.then_inc(kv_done, 1)

                def attend(b, p):
                    free_bank(m_read, BANK_M, M_OUT, b)
                    pe.wait_ge(kv_set, b + 1)
                    pe.wait_ge(eqlo_set[0], b + 1)
                    pe.wait_ge(eqlo_set[1], b + 1)
                    for t in range(2):
                        for j in range(8):
                            f = slice(256 * (j % 4) + P * t, 256 * (j % 4) + P * t + P)
                            n = 0
                            for e in (bf_hi(eq[:, p, j // 4, f]), eq_lo[:, p, j // 4, f]):
                                for c in range(3):
                                    last = mm(m_out[:, t, j, :], e, kvp[:, c, j, :], start=(t + j + n == 0),
                                              stop=False, skip_group_check=True)
                                    n += 1
                    last.then_inc(o_done, 1)

                def w_out(b, p):
                    pe.wait_ge(t_read, reads_before(BANK_T, T_ATT, b) + 1)
                    free_bank(q_read, BANK_Q, Q_WOUT, b)
                    for t in range(2):
                        c = slice(P * t, P * t + P)
                        last = three(bQ[:, t, 384:512], atT[:, 0, c], atT[:, 1, c], wa_hi[:, 384:512],
                                     wa_lo[:, 384:512], True)
                    last.then_inc(w_done, 1)

                def router(b, p):
                    pe.wait_ge(t_read, reads_before(BANK_T, T_LN2, b) + 1)
                    free_bank(m_read, BANK_M, M_RT, b)
                    for t in range(2):
                        c = slice(P * t, P * t + P)
                        last = three(m_rt[:, t, :], x2T[:, 0, c], x2T[:, 1, c], wa_hi[:, 512:520], wa_lo[:, 512:520],
                                     t == 0)
                    last.then_inc(rt_done, 1)

                def positions(b, p):
                    pe.wait_ge(both_set, b + 1)
                    need(pe, cum_set, b)
                    free_bank(m_read, BANK_M, M_POS, b)
                    mm(m_pos[:, 0, :], tri[:], both[:, p, 0, :], start=True, stop=False, skip_group_check=True)
                    mm(m_pos[:, 0, :], ones[:], mcum[:], start=False, stop=True, skip_group_check=True)
                    mm(m_pos[:, 1, :], tri[:], both[:, p, 1, :], start=False, stop=False, skip_group_check=True)
                    mm(m_pos[:, 1, :], ones[:], mcum[:], start=False, stop=False, skip_group_check=True)
                    mm(m_pos[:, 1, :], ones[:], both[:, p, 0, :], start=False, stop=True,
                       skip_group_check=True).then_inc(pos_done, 1)

                pipeline(pe, [(3, attend), (2, ext_turn(0, T_EXTQ, t_extq)), (4, ln2_turn), (2, features(0)),
                              (4, router), (3, att_turn), (2, features(1)), (2, ext_turn(1, T_EXTK, t_extk)),
                              (3, w_out), (1, ln1_turn), (2, features(2)), (1, qkv), (2, features(3)), (2, kv),
                              (4, positions)])

                pe.wait_ge(cum_set, NB)
                need(pe, m_read, reads_before(BANK_M, M_OUT, NB + LAG))
                mm(bM[:, 0:E], ones[:], mcum[:], start=True, stop=True, skip_group_check=True).then_inc(cnt_done, 1)

                w_h = w_hi[:].rearrange("p (e w n) -> p e w n", e=E, w=3)
                w_l = w_lo[:].rearrange("p (e w n) -> p e w n", e=E, w=3)
                expert = {}

                def rows_turn(t, p):
                    pe.wait_ge(xl_load[p], 8 * (t - p) + 16)
                    need(pe, xlT_set, t)
                    turn(lambda n: xl[:, p, n % 2, D * (n // 2):D * (n // 2) + D], 4).then_inc(xl_turned, 1)

                def load_expert(t):
                    return nc.values_load(tab[0:1, 0, bass.ds(t, 1)], engines=[mybir.EngineType.PE], min_val=0,
                                          max_val=E - 1, skip_runtime_bounds_check_because="clamped to the last expert")

                def hidden(k):
                    def stage(t, p):
                        if k == 0:
                            expert[1] = load_expert(t)
                            pe.wait_ge(xlT_set, t + 1)
                        e = expert[1]
                        need(pe, act_set, 2 * t + k - 1)
                        for b in range(2):
                            for w in range(2):
                                c = slice(256 * k + P * b, 256 * k + P * b + P)
                                o = z[:, k, 512 * b + 256 * w:512 * b + 256 * w + 256]
                                mm(o, w_h[:, bass.ds(e, 1), w, c].rearrange("p o n -> p (o n)"), xlT[:, p, 0, :],
                                   start=(w == 0), stop=False, skip_group_check=True)
                                mm(o, w_h[:, bass.ds(e, 1), w, c].rearrange("p o n -> p (o n)"), xlT[:, p, 1, :],
                                   start=False, stop=False, skip_group_check=True)
                                last = mm(o, w_l[:, bass.ds(e, 1), w, c].rearrange("p o n -> p (o n)"),
                                          xlT[:, p, 0, :], start=False, stop=True, skip_group_check=True)
                        last.then_inc(h_done, 1)
                    return stage

                def output(t, p):
                    e = load_expert(t)
                    pe.wait_ge(actlo_set, 2 * (t + 1))
                    need(pe, y_set, 3 * (t - 1))
                    for h in range(2):
                        o = bQ[:, p, P * h:P * h + P]
                        c = slice(P * h, P * h + P)
                        for b in range(4):
                            w = slice(P * b, P * b + P)
                            w2h = w_h[:, bass.ds(e, 1), 2, w].rearrange("p o n -> p (o n)")
                            w2l = w_l[:, bass.ds(e, 1), 2, w].rearrange("p o n -> p (o n)")
                            mm(o, act_hi[:, p, b, c], w2h, start=(h + b == 0), stop=False, skip_group_check=True)
                            mm(o, act_hi[:, p, b, c], w2l, start=False, stop=False, skip_group_check=True)
                            last = mm(o, act_lo[:, p, b, c], w2h, start=False, stop=True, skip_group_check=True)
                    last.then_inc(y_done, 1)

                pe.wait_ge(tab_set, 1)
                pe.wait_ge(wsplit_lo, NB)
                need(pe, z_exp, 4 * NB)
                need(pe, t_read, reads_before(BANK_T, T_EXTQ, NB + LAG))
                need(pe, q_read, 2 * NB)
                pipeline(pe, [(0, rows_turn), (1, hidden(0)), (1, hidden(1)), (2, output)], 2, NX)


def kernel(L0_attn_x, L0_attn_w_qkv, L0_attn_w_out, L0_attn_b_out, L0_attn_random_features, L0_ffn_gate_w, L0_ffn_w1,
           L0_ffn_w3, L0_ffn_w2):
    import numpy as np
    import concourse.bacc as bacc
    from concourse.bass_utils import run_bass_kernel_spmd

    cont = np.ascontiguousarray
    wa = np.concatenate([np.asarray(w).T for w in (L0_attn_w_qkv, L0_attn_w_out, L0_ffn_gate_w)], axis=1)
    w13 = [np.asarray(w).transpose(2, 0, 1) for w in (L0_ffn_w1, L0_ffn_w3)]
    w2 = np.asarray(L0_ffn_w2).transpose(2, 0, 1).reshape(4, P, E, D).transpose(1, 2, 0, 3).reshape(P, E, 4 * D)
    features_w = np.zeros((P, 4 * F), np.float32)
    for h in range(4):
        for part in range(3):
            r0 = 32 * part + HD * h
            features_w[r0:r0 + HD, F * h:F * h + F] = np.asarray(L0_attn_random_features).T
        for part in range(2):
            features_w[96 + 4 * part + h, F * h:F * h + F] = -8.0
    mask = np.zeros((P, 18), np.float32)
    for r in range(P):
        mask[r, HD * (r // F):HD * (r // F) + HD] = 1.0
        mask[r, 16 + r // F] = 1.0
    arrays = {
        "x": cont(np.asarray(L0_attn_x).reshape(T, D)),
        "wa": cont(wa),
        "bout": cont(np.broadcast_to(np.asarray(L0_attn_b_out), (P, D))),
        "features_w": features_w,
        "wffn": cont(np.concatenate([*w13, w2], axis=2).reshape(P, E * 3 * HID)),
        "mask": mask,
    }
    nc = bacc.Bacc("TRN2", target_bir_lowering=False, num_devices=1)
    ins = {n: nc.dram_tensor(n, a.shape, F32, kind="ExternalInput").ap() for n, a in arrays.items()}
    out = nc.dram_tensor("out", (T, D), F32, kind="ExternalOutput").ap()
    xs = nc.dram_tensor("xs", (E * CAP + SLOTS, ROW // 2), mybir.dt.int32, kind="Internal").ap()
    ins["x"] = ins["x"].rearrange("(t p) d -> p t d", p=P)
    build(nc, **ins, out=out, xs=xs)
    r = run_bass_kernel_spmd(nc, [arrays], core_ids=[0])
    return r.results[0]["out"].reshape(L0_attn_x.shape)
```
